# Optimizing a Trainium2 kernel written in Bass

```python
import numpy as np
import jax
import jax.numpy as jnp

def _softmax(x, axis=-1):
    return jax.nn.softmax(x, axis=axis)

def _gelu(x):
    return jax.nn.gelu(x, approximate=True)

def _silu(x):
    return jax.nn.silu(x)

def _sigmoid(x):
    return jax.nn.sigmoid(x)

def _layernorm(x, axis=-1, eps=1e-05):
    m = jnp.mean(x, axis=axis, keepdims=True)
    v = jnp.var(x, axis=axis, keepdims=True)
    return (x - m) / jnp.sqrt(v + eps)

def _scatter_add(tgt, idx, src, axis=0):
    return tgt.at[idx].add(src)

def _segment_sum(src, seg, n):
    return jax.ops.segment_sum(src, seg, n)
kernel_name = 'mk_gnn_resnorm_d1_gnn_r8_069b1b'

def setup_inputs(seed: int=0):
    np.random.seed(seed)
    _w = jnp.asarray

    def _rec_inputs():
        import jax
        import jax.numpy as jnp
        _gk = jax.random.key(seed)
        x = -0.000202 + 1 * jax.random.normal(jax.random.fold_in(_gk, 1), (12500, 64), jnp.float32)
        src = jax.random.randint(jax.random.fold_in(_gk, 2), (400000,), 0, 12500, jnp.int32)
        dst = jnp.minimum((12500 * jax.random.uniform(jax.random.fold_in(_gk, 3), (400000,)) ** 2.0).astype(jnp.int32), 99999)
        _o = jnp.argsort(dst, stable=True)
        src = src[_o]
        dst = dst[_o]
        edge_attr_41 = -0.000138925 + 0.999911 * jax.random.normal(jax.random.fold_in(_gk, 12), (400000, 41), jnp.float32)
        return (x, src, dst, edge_attr_41)
    x, src, dst, edge_attr_41 = _rec_inputs()

    def _L0_gnn_setup():
        import jax, jax.numpy as jnp
        import numpy as np
        N_NODES = 12500
        N_EDGES = 150000
        NODE_F = 64
        EDGE_F = 41
        EPS = 1e-05

        def _bn(x, gamma, beta):
            m = x.mean(axis=0)
            v = x.var(axis=0)
            return gamma * (x - m) * jax.lax.rsqrt(v + EPS) + beta
        key = jax.random.key(seed)
        ks = jax.random.split(key, 12)
        cat = 2 * NODE_F + EDGE_F
        return {'node_feats': jax.random.normal(ks[0], (N_NODES, NODE_F), dtype=jnp.float32), 'edge_feats': jax.random.normal(ks[1], (N_EDGES, EDGE_F), dtype=jnp.float32), 'src': jax.random.randint(ks[2], (N_EDGES,), 0, N_NODES, dtype=jnp.int32), 'dst': jax.random.randint(ks[3], (N_EDGES,), 0, N_NODES, dtype=jnp.int32), 'W1': jax.random.normal(ks[4], (NODE_F, cat), dtype=jnp.float32) / np.sqrt(cat), 'b1': jnp.zeros((NODE_F,), dtype=jnp.float32), 'W2': jax.random.normal(ks[5], (NODE_F, cat), dtype=jnp.float32) / np.sqrt(cat), 'b2': jnp.zeros((NODE_F,), dtype=jnp.float32), 'g1': jnp.ones((NODE_F,), dtype=jnp.float32), 'bt1': jnp.zeros((NODE_F,), dtype=jnp.float32), 'g2': jnp.ones((NODE_F,), dtype=jnp.float32), 'bt2': jnp.zeros((NODE_F,), dtype=jnp.float32), 'g3': jnp.ones((NODE_F,), dtype=jnp.float32), 'bt3': jnp.zeros((NODE_F,), dtype=jnp.float32)}
    _L0_gnn_all = _L0_gnn_setup()
    _L0_gnn_in = {k: v for k, v in _L0_gnn_all.items() if k in ('W1', 'b1', 'W2', 'b2', 'g1', 'bt1', 'g2', 'bt2', 'g3', 'bt3')}
    del _L0_gnn_all
    return {'x': x, 'src': src, 'dst': dst, 'edge_attr_41': edge_attr_41, 'L0_gnn_W1': _L0_gnn_in['W1'], 'L0_gnn_b1': _L0_gnn_in['b1'], 'L0_gnn_W2': _L0_gnn_in['W2'], 'L0_gnn_b2': _L0_gnn_in['b2'], 'L0_gnn_g1': _L0_gnn_in['g1'], 'L0_gnn_bt1': _L0_gnn_in['bt1'], 'L0_gnn_g2': _L0_gnn_in['g2'], 'L0_gnn_bt2': _L0_gnn_in['bt2'], 'L0_gnn_g3': _L0_gnn_in['g3'], 'L0_gnn_bt3': _L0_gnn_in['bt3']}

def reference(x, src, dst, edge_attr_41, L0_gnn_W1, L0_gnn_b1, L0_gnn_W2, L0_gnn_b2, L0_gnn_g1, L0_gnn_bt1, L0_gnn_g2, L0_gnn_bt2, L0_gnn_g3, L0_gnn_bt3):
    import jax
    import jax.numpy as jnp

    def _L0_gnn_ref(node_feats, edge_feats, src, dst, W1, b1, W2, b2, g1, bt1, g2, bt2, g3, bt3):
        import jax, jax.numpy as jnp
        import numpy as np
        N_NODES = 12500
        N_EDGES = 150000
        NODE_F = 64
        EDGE_F = 41
        EPS = 1e-05

        def _bn(x, gamma, beta):
            m = x.mean(axis=0)
            v = x.var(axis=0)
            return gamma * (x - m) * jax.lax.rsqrt(v + EPS) + beta
        total_edge = jnp.concatenate([node_feats[src], node_feats[dst], edge_feats], axis=-1)
        nbr_filter = jax.nn.sigmoid(_bn(total_edge @ W1.T + b1, g1, bt1))
        nbr_core = jax.nn.softplus(_bn(nbr_filter, g2, bt2))
        h = nbr_filter * nbr_core
        agg = jax.ops.segment_sum(h, dst, num_segments=N_NODES)
        new_node = _bn(agg, g3, bt3)
        return node_feats + new_node
    x = _layernorm(x + _L0_gnn_ref(x, edge_attr_41, src, dst, L0_gnn_W1, L0_gnn_b1, L0_gnn_W2, L0_gnn_b2, L0_gnn_g1, L0_gnn_bt1, L0_gnn_g2, L0_gnn_bt2, L0_gnn_g3, L0_gnn_bt3), axis=-1)
    return x

_drawn_inputs = setup_inputs


def setup_inputs(seed=0):
    import zlib

    import numpy as np

    out = dict(_drawn_inputs(seed))
    spreads = {'L0_gnn_b1': (0.0, 0.8),
     'L0_gnn_b2': (0.0, 0.1),
     'L0_gnn_g1': (1.0, 0.6),
     'L0_gnn_bt1': (0.0, 0.8),
     'L0_gnn_g2': (1.0, 0.6),
     'L0_gnn_bt2': (0.0, 0.8),
     'L0_gnn_g3': (1.0, 0.2),
     'L0_gnn_bt3': (0.0, 0.1)}
    factors = {}
    for name, (base, spread) in spreads.items():
        noise = np.random.default_rng([zlib.crc32(name.encode()), seed]).standard_normal(out[name].shape)
        drawn = base * np.exp(spread * noise) if base else spread * noise
        out[name] = jnp.asarray(drawn.astype(out[name].dtype))
    for name, factor in factors.items():
        out[name] = (out[name] * factor).astype(out[name].dtype)
    return out
```

```python
import concourse.bass as bass
from concourse import mybir
from contextlib import ExitStack

NODES, EDGES, D, EF = 12500, 400000, 64, 41
P = 128
TS = 8
SUP = TS * P
SR = 4
COLS = SUP // 2
RC = SR * COLS
TILES = EDGES // P
ROUNDS = -(-EDGES // (SR * SUP))
SUPERS = ROUNDS * SR
ALL_TILES = SUPERS * TS
PAD_EDGES = SUPERS * SUP
LAST = TILES // TS
LAST_TILES = TILES - LAST * TS
NB = -(-NODES // P)
PAD_NODES = NB * P
GT = 4
GROUPS = ALL_TILES // GT
WIN = 64
AGG_COLS = PAD_NODES + 2 * WIN
KF = 112
EPS = 1e-5

f32 = mybir.dt.float32
bf16 = mybir.dt.bfloat16
i32 = mybir.dt.int32
ALU = mybir.AluOpType
ACT = mybir.ActivationFunctionType
AX = mybir.AxisListType

EXP_MAX = 1e18
FB = 7
EDGE_BLOCKS = 3


def real_tiles(s):
    return max(0, min(TS, TILES - s * TS))


def gnn_kernel(nc, xT, xn, src_cols, dst_cols, dst_rows, edgeT, w_edge, w_dst, params, wcol,
               ident_in, fold_in, nodecol_in, iota_in, out):
    ctx = ExitStack()
    with ctx:
        def sb(name, shape, dt=f32, c=ctx):
            return c.enter_context(nc.sbuf_tensor(name, shape, dt))

        def pb(name, shape, c, dt=f32):
            return c.enter_context(nc.psum_tensor(name, shape, dt))

        def sem(name, c=ctx):
            return c.enter_context(nc.semaphore(name))

        z_dram = nc.dram_tensor("z_dram", [ROUNDS, P, RC], f32).ap()
        f_dram = nc.dram_tensor("f_dram", [ROUNDS, P, RC], f32).ap()
        gmin_dram = nc.dram_tensor("gmin_dram", [ROUNDS, GROUPS // ROUNDS], i32).ap()
        gmax_dram = nc.dram_tensor("gmax_dram", [ROUNDS, GROUPS // ROUNDS], i32).ap()
        blk_dram = nc.dram_tensor("blk_dram", [ROUNDS, SR, 2], i32).ap()
        span_dram = nc.dram_tensor("span_dram", [ROUNDS, 1], i32).ap()

        ident = sb("ident", [P, P])
        fold = sb("fold", [P, P])
        par = sb("par", [P, 6])
        wc = sb("wc", [P, 1])
        gmin_row = sb("gmin_row", [1, GROUPS], i32)
        gmax_row = sb("gmax_row", [1, GROUPS], i32)
        span_row = sb("span_row", [1, ROUNDS], i32)
        dst_rel = sb("dst_rel", [P, ALL_TILES])
        coef1 = sb("coef1", [P, 2])
        coef2 = sb("coef2", [P, 2])
        stats = sb("stats", [P, LAST + 1, 6])
        iota = sb("iota", [P, WIN])

        p1 = ExitStack()
        with p1:
            blk_row = sb("blk_row", [1, 2 * SUPERS], i32, p1)
            w_e = sb("w_e", [KF, D], f32, p1)
            nodecol = sb("nodecol", [P, NB], f32, p1)
            pd = sb("pd", [P, NB, EDGE_BLOCKS, D], bf16, p1)

            c0 = ExitStack()
            with c0:
                xT_s = sb("xT_s", [D, PAD_NODES], f32, c0)
                w_d = sb("w_d", [D, D], f32, c0)
                dst_r = sb("dst_r", [ROUNDS, SR * SUP], i32, c0)
                dst_c = sb("dst_c", [P, ALL_TILES], i32, c0)
                gmin_b = sb("gmin_b", [P, GROUPS], i32, c0)
                gm = sb("gm", [ROUNDS, 2, GROUPS // ROUNDS], i32, c0)
                bl = sb("bl", [ROUNDS, SR, 2], i32, c0)
                bs = sb("bs", [ROUNDS, SR, 2], i32, c0)
                dif = sb("dif", [ROUNDS, GROUPS // ROUNDS], i32, c0)
                span = sb("span", [ROUNDS, 1], i32, c0)
                rest = sb("rest", [P, 2, 512], f32, c0)
                ps = [pb(f"ps_pd{i}", [P, 512], c0) for i in range(2)]
                s_x, s_dr, s_dc, s_c, s_tab, s_row, s_gb = (
                    sem(n, c0) for n in ("s_x", "s_dr", "s_dc", "s_c", "s_tab", "s_row", "s_gb"))
                pd_mm, pd_used, rng, split = (sem(n, c0) for n in ("pd_mm", "pd_used", "rng", "split"))
                KB = 8
                banks = [(b, min(KB, NB - b)) for b in range(0, NB, KB)]
                c0b = c0.enter_context(nc.Block())

                @c0b.sync
                def _(sp):
                    sp.dma_start(dst_r[:], dst_rows).then_inc(s_dr, 16)
                    sp.dma_start(w_d[:], w_dst).then_inc(s_x, 16)
                    sp.dma_start(xT_s[:], xT).then_inc(s_x, 16)
                    sp.dma_start(dst_c[:], dst_cols).then_inc(s_dc, 16)
                    for t, s in ((ident, ident_in), (fold, fold_in), (par, params), (wc, wcol),
                                 (w_e, w_edge), (nodecol, nodecol_in), (iota, iota_in)):
                        sp.dma_start(t[:], s).then_inc(s_c, 16)
                    sp.wait_ge(rng, 6)
                    sp.dma_start(gmin_dram, gm[:, 0, :]).then_inc(s_tab, 16)
                    sp.dma_start(gmax_dram, gm[:, 1, :]).then_inc(s_tab, 16)
                    sp.dma_start(blk_dram, bs[:]).then_inc(s_tab, 16)
                    sp.dma_start(span_dram, span[:]).then_inc(s_tab, 16)
                    sp.wait_ge(s_tab, 64)
                    sp.dma_start(gmin_b[:], gmin_dram.rearrange("r g -> (r g)").partition_broadcast(P)
                                 ).then_inc(s_gb, 16)
                    for t, s, e in ((gmin_row, gmin_dram, "r g -> (r g)"), (gmax_row, gmax_dram, "r g -> (r g)"),
                                    (blk_row, blk_dram, "r s t -> (r s t)"), (span_row, span_dram, "r o -> (r o)")):
                        sp.dma_start(t[:], s.rearrange(e)[None, :]).then_inc(s_row, 16)
                    sp.wait_ge(s_row, 64)
                    sp.wait_ge(s_c, 112)

                @c0b.tensor
                def _(pe):
                    pe.wait_ge(s_x, 32)
                    for i, (b0, n) in enumerate(banks):
                        if i >= 2:
                            pe.wait_ge(pd_used, i - 1)
                        for k in range(n):
                            m = nc.tensor.matmul(ps[i % 2][:, k * D:(k + 1) * D],
                                                 xT_s[:, (b0 + k) * P:(b0 + k + 1) * P], w_d[:],
                                                 start=True, stop=True)
                        m.then_inc(pd_mm, 1)

                @c0b.vector
                def _(dve):
                    dve.wait_ge(s_dr, 16)
                    by_group = dst_r[:].rearrange("r (g e) -> r g e", e=GT * P)
                    nc.vector.tensor_reduce(gm[:, 0, :], by_group, AX.X, ALU.min).then_inc(rng, 1)
                    nc.vector.tensor_reduce(gm[:, 1, :], by_group, AX.X, ALU.max).then_inc(rng, 1)
                    dve.wait_ge(rng, 2)
                    pairs = gm[:].rearrange("r m (s g) -> r m s g", g=TS // GT)
                    nc.vector.tensor_tensor(bl[:, :, 0], pairs[:, 0, :, 0], pairs[:, 0, :, 1],
                                            ALU.min).then_inc(rng, 1)
                    nc.vector.tensor_tensor(bl[:, :, 1], pairs[:, 1, :, 0], pairs[:, 1, :, 1],
                                            ALU.max).then_inc(rng, 1)
                    nc.vector.tensor_tensor(dif[:], gm[:, 1, :], gm[:, 0, :], ALU.subtract).then_inc(split, 1)
                    dve.wait_ge(rng, 4)
                    nc.vector.tensor_single_scalar(bs[:], bl[:], 7, ALU.arith_shift_right).then_inc(rng, 1)
                    dve.wait_ge(split, 1)
                    nc.vector.tensor_reduce(span[:], dif[:], AX.X, ALU.max).then_inc(rng, 1)
                    n_split = 1
                    for i, (b0, n) in enumerate(banks):
                        dve.wait_ge(pd_mm, i + 1)
                        v = ps[i % 2][:, 0:n * D].rearrange("p (b d) -> p b d", d=D)
                        r = [rest[:, j, 0:n * D].rearrange("p (b d) -> p b d", d=D) for j in range(2)]
                        o = pd[:, b0:b0 + n, :, :]
                        nc.vector.tensor_copy(o[:, :, 0, :], v).then_inc(split, 1)
                        dve.wait_ge(split, n_split + 1)
                        nc.vector.tensor_tensor(r[0], v, o[:, :, 0, :], ALU.subtract).then_inc(split, 1)
                        dve.wait_ge(split, n_split + 2)
                        nc.vector.tensor_copy(o[:, :, 1, :], r[0]).then_inc(split, 1)
                        dve.wait_ge(split, n_split + 3)
                        nc.vector.tensor_tensor(r[1], r[0], o[:, :, 1, :], ALU.subtract).then_inc(pd_used, 1)
                        dve.wait_ge(pd_used, i + 1)
                        nc.vector.tensor_copy(o[:, :, 2, :], r[1]).then_inc(split, 1)
                        dve.wait_ge(split, n_split + 4)
                        n_split += 4
                    dve.wait_ge(s_gb, 16)
                    dve.wait_ge(s_dc, 16)
                    g3 = gmin_b[:].rearrange("p (g o) -> p g o", o=1).to_broadcast([P, GROUPS, GT])
                    nc.vector.tensor_tensor(dst_rel[:].rearrange("p (g t) -> p g t", t=GT),
                                            dst_c[:].rearrange("p (g t) -> p g t", t=GT), g3,
                                            ALU.subtract)

            c1 = ExitStack()
            with c1:
                src_ix = sb("src_ix", [P, SR, TS], i32, c1)
                G = sb("G", [P, SR, TS, D], f32, c1)
                xe = sb("xe", [KF, SR, SUP], f32, c1)
                dst_b = sb("dst_b", [P, SR, SUP], i32, c1)
                one_t = sb("one_t", [P, 2, SUP], bf16, c1)
                zs = sb("zs", [P, 2, COLS], f32, c1)
                zt = sb("zt", [P, SR, COLS], f32, c1)
                zero = sb("zero", [P, COLS], bf16, c1)
                ps_x = [pb(f"ps_x{i}", [D, SUP], c1) for i in range(2)]
                ps_z = [pb(f"ps_z{i}", [P, COLS], c1) for i in range(2)]
                ps_t = [pb(f"ps_t{i}", [P, COLS], c1) for i in range(2)]
                gathered = [sem(f"gathered{i}", c1) for i in range(SR)]
                src_in = [sem(f"src_in{i}", c1) for i in range(SR)]
                edge_in = [sem(f"edge_in{i}", c1) for i in range(SR)]
                dst_in = [sem(f"dst_in{i}", c1) for i in range(SR)]
                z_out = [sem(f"z_out{i}", c1) for i in range(SR)]
                (zeroed, one_ready, one_used, g_turned, xe_ready, z_done, zs_ready, z_turned, zt_ready,
                 counted, passed) = (sem(n, c1) for n in (
                     "zeroed", "one_ready", "one_used", "g_turned", "xe_ready", "z_done", "zs_ready",
                     "z_turned", "zt_ready", "counted", "passed"))
                b1 = c1.enter_context(nc.Block())

                def rounds(eng, body):
                    body(0, True, False)
                    with eng.Fori(1, ROUNDS - 1) as r:
                        body(r, False, False)
                    body(ROUNDS - 1, False, True)

                @b1.gpsimd
                def _(pool):
                    def body(r, first, last):
                        for q in range(SR):
                            if not first:
                                pool.wait_ge(g_turned, r * SR + q - SR + 1)
                            pool.wait_ge(src_in[q], (r + 1) * 16)
                            pool.sem_inc(passed, 1)
                            for t in range(TS):
                                nc.gpsimd.indirect_dma_start(
                                    out=G[:, q, t, :], out_offset=None, in_=xn,
                                    in_offset=bass.IndirectOffsetOnAxis(ap=src_ix[:, q, t:t + 1], axis=0),
                                ).then_inc(gathered[q], 16)
                    rounds(pool, body)

                @b1.sync
                def _(sp):
                    def body(r, first, last):
                        for q in range(SR):
                            s = r * SR + q
                            if not first:
                                sp.wait_ge(gathered[q], r * (16 * TS))
                            sp.dma_start(src_ix[:, q, :], src_cols[bass.ds(s, 1), :, :].rearrange(
                                "o p t -> (o p) t")).then_inc(src_in[q], 16)
                            if not first:
                                sp.wait_ge(z_done, s - SR + 1)
                            sp.dma_start(xe[D:KF, q, :], edgeT[bass.ds(s, 1), :, :].rearrange("o k e -> (o k) e")
                                         ).then_inc(edge_in[q], 16)
                            if not first:
                                sp.wait_ge(zs_ready, s - SR + 1)
                            sp.sem_inc(passed, 1)
                            sp.dma_start(dst_b[:, q, :],
                                         dst_rows[bass.ds(r, 1), q * SUP:(q + 1) * SUP].rearrange(
                                             "o e -> (o e)").partition_broadcast(P)).then_inc(dst_in[q], 16)
                    rounds(sp, body)

                @b1.vector
                def _(dve):
                    nc.vector.memset(zero[:], 0.0).then_inc(zeroed, 1)
                    made = dve.alloc_register("marks_made")
                    before = dve.alloc_register("marks_before")
                    dve.reg_mov(made, 1)
                    dve.reg_mov(before, 1)

                    def body(r, first, last):
                        for q in range(SR):
                            s = r * SR + q
                            lo = dve.value_load(blk_row[0:1, bass.ds(s * 2, 1)], min_val=0, max_val=NB - 1)
                            hi = dve.value_load(blk_row[0:1, bass.ds(s * 2 + 1, 1)], min_val=0, max_val=NB - 1)
                            dve.wait_ge(dst_in[q], (r + 1) * 16)
                            dve.sem_inc(passed, 1)
                            dve.wait_ge(one_used, dve.snap(before, min_val=1))
                            dve.sem_inc(passed, 1)
                            dve.reg_mov(before, made)
                            with dve.Fori(lo, hi + 1) as b:
                                nc.vector.tensor_scalar(one_t[:, q % 2, :], dst_b[:, q, :],
                                                        nodecol[:, bass.ds(b, 1)], None,
                                                        ALU.is_equal).then_inc(one_ready, 1)
                                dve.reg_add(made, made, 1)
                                dve.wait_ge(one_used, dve.snap(made, min_val=1))
                            dve.wait_ge(z_done, s + 1)
                            if not first or q >= 2:
                                dve.wait_ge(z_turned, s - 1)
                            nc.vector.tensor_copy(zs[:, q % 2, :], ps_z[q % 2][:]).then_inc(zs_ready, 1)
                            dve.wait_ge(zt_ready, s + 1)
                            if not last or s < LAST:
                                nc.vector.bn_stats(stats[:, bass.ds(s, 1), :], zt[:, q, :]).then_inc(counted, 1)
                            elif s == LAST:
                                even, odd = -(-LAST_TILES // 2) * P, LAST_TILES // 2 * P
                                nc.vector.bn_stats(stats[0:D, s, :], zt[0:D, q, 0:even])
                                nc.vector.bn_stats(stats[D:P, s, :], zt[D:P, q, 0:odd]).then_inc(counted, 1)
                    rounds(dve, body)

                @b1.tensor
                def _(pe):
                    pe.wait_ge(zeroed, 1)
                    pe.sem_inc(one_used, 1)
                    seen = pe.alloc_register("marks_seen")
                    pe.reg_mov(seen, 0)

                    def body(r, first, last):
                        for q in range(SR):
                            s = r * SR + q
                            lo = pe.value_load(blk_row[0:1, bass.ds(s * 2, 1)], min_val=0, max_val=NB - 1)
                            hi = pe.value_load(blk_row[0:1, bass.ds(s * 2 + 1, 1)], min_val=0, max_val=NB - 1)
                            z = ps_z[q % 2]
                            if not first or q >= 2:
                                pe.wait_ge(zs_ready, s - 1)
                            nc.tensor.matmul(z[:], zero[:, 0:P], zero[:], start=True, stop=False)
                            with pe.Fori(lo, hi + 1) as b:
                                pe.reg_add(seen, seen, 1)
                                pe.wait_ge(one_ready, pe.snap(seen, min_val=1))
                                for t in range(TS):
                                    for part in range(EDGE_BLOCKS):
                                        m = nc.tensor.matmul(
                                            z[:, t * D:(t + 1) * D], one_t[:, q % 2, t * P:(t + 1) * P],
                                            pd[:, bass.ds(b, 1), part, :].rearrange("p o d -> p (o d)"),
                                            start=False, stop=False)
                                m.then_inc(one_used, 1)
                            pe.wait_ge(gathered[q], (r + 1) * (16 * TS))
                            if not first or q >= 2:
                                pe.wait_ge(xe_ready, s - 1)
                            pe.sem_inc(passed, 1)
                            for t in range(TS):
                                m = nc.tensor.transpose(ps_x[q % 2][:, t * P:(t + 1) * P], G[:, q, t, :], ident[:])
                            m.then_inc(g_turned, 1)
                            pe.wait_ge(xe_ready, s + 1)
                            pe.wait_ge(edge_in[q], (r + 1) * 16)
                            for t in range(TS):
                                m = nc.tensor.matmul(z[:, t * D:(t + 1) * D], xe[:, q, t * P:(t + 1) * P],
                                                     w_e[:], start=False, stop=(t == TS - 1))
                            m.then_inc(z_done, 1)
                            pe.wait_ge(zs_ready, s + 1)
                            if not first or q >= 2:
                                pe.wait_ge(zt_ready, s - 1)
                            for k in range(TS // 2):
                                m = nc.tensor.transpose(ps_t[q % 2][:, k * P:(k + 1) * P],
                                                        zs[:, q % 2, k * P:(k + 1) * P], ident[:])
                            m.then_inc(z_turned, 1)
                    rounds(pe, body)

                @b1.scalar
                def _(act):
                    def body(r, first, last):
                        for q in range(SR):
                            s = r * SR + q
                            act.wait_ge(g_turned, s + 1)
                            if not first:
                                act.wait_ge(z_done, s - SR + 1)
                            nc.scalar.copy(xe[0:D, q, :], ps_x[q % 2][:]).then_inc(xe_ready, 1)
                            act.wait_ge(z_turned, s + 1)
                            if not first:
                                act.wait_ge(z_out[q], r * 16)
                                act.wait_ge(counted, s - SR + 1)
                            nc.scalar.copy(zt[:, q, :], ps_t[q % 2][:]).then_inc(zt_ready, 1)
                            act.wait_ge(zt_ready, s + 1)
                            act.dma_start(z_dram[bass.ds(r, 1), :, q * COLS:(q + 1) * COLS].rearrange(
                                "o p c -> (o p) c"), zt[:, q, :]).then_inc(z_out[q], 16)
                    rounds(act, body)
                    for q in range(SR):
                        act.wait_ge(z_out[q], ROUNDS * 16)

        def coefficients(name, coef, gamma, beta):
            c = ExitStack()
            with c:
                v = sb(name + "_v", [P, 12], f32, c)
                ps = pb(name + "_ps", [P, 2], c)
                done, summed, rooted = sem(name + "_done", c), sem(name + "_summed", c), sem(name + "_rooted", c)
                blk = c.enter_context(nc.Block())

                @blk.vector
                def _(dve):
                    n = [0]

                    def then(i):
                        n[0] += 1
                        i.then_inc(done, 1)
                        dve.wait_ge(done, n[0])

                    nc.vector.memset(v[:, 2:12], 0.0)
                    then(nc.vector.bn_aggr(v[:, 0:2], stats[:].rearrange("p s k -> p (s k)")))
                    then(nc.vector.tensor_tensor(v[:, 2:3], v[:, 0:1], wc[:], ALU.mult))
                    dve.wait_ge(summed, 1)
                    then(nc.vector.tensor_copy(v[:, 3:4], ps[:, 0:1]))
                    then(nc.vector.tensor_tensor(v[:, 4:5], v[:, 0:1], v[:, 3:4], ALU.subtract))
                    then(nc.vector.tensor_tensor(v[:, 5:6], v[:, 4:5], v[:, 4:5], ALU.mult))
                    then(nc.vector.tensor_tensor(v[:, 6:7], v[:, 5:6], v[:, 1:2], ALU.add))
                    then(nc.vector.tensor_tensor(v[:, 7:8], v[:, 6:7], wc[:], ALU.mult))
                    dve.wait_ge(summed, 2)
                    then(nc.vector.tensor_scalar(v[:, 8:9], ps[:, 1:2], EPS, None, ALU.add))
                    dve.wait_ge(rooted, 1)
                    then(nc.vector.reciprocal(v[:, 10:11], v[:, 9:10]))
                    then(nc.vector.tensor_tensor(coef[:, 0:1], v[:, 10:11], par[:, gamma:gamma + 1], ALU.mult))
                    then(nc.vector.tensor_tensor(v[:, 11:12], v[:, 3:4], coef[:, 0:1], ALU.mult))
                    then(nc.vector.tensor_tensor(coef[:, 1:2], par[:, beta:beta + 1], v[:, 11:12], ALU.subtract))

                @blk.tensor
                def _(pe):
                    pe.wait_ge(done, 2)
                    nc.tensor.matmul(ps[:, 0:1], fold[:], v[:, 2:3], start=True, stop=True).then_inc(summed, 1)
                    pe.wait_ge(done, 7)
                    nc.tensor.matmul(ps[:, 1:2], fold[:], v[:, 7:8], start=True, stop=True).then_inc(summed, 1)

                @blk.scalar
                def _(act):
                    act.wait_ge(done, 8)
                    nc.scalar.activation(v[:, 9:10], v[:, 8:9], ACT.Sqrt).then_inc(rooted, 1)

        coefficients("bn1", coef1, 0, 1)

        c2 = ExitStack()
        with c2:
            fz = sb("fz", [P, FB, RC], f32, c2)
            z_in = [sem(f"z_in{i}", c2) for i in range(FB)]
            f_out = [sem(f"f_out{i}", c2) for i in range(FB)]
            f_ready, f_counted, passed2 = sem("f_ready", c2), sem("f_counted", c2), sem("passed2", c2)
            LOOPS = ROUNDS // FB
            AHEAD = 4
            b2 = c2.enter_context(nc.Block())

            def in_turns(eng, body):
                body(0, True, False)
                with eng.Fori(1, LOOPS - 1) as r:
                    body(r, False, False)
                body(LOOPS - 1, False, True)

            @b2.sync
            def _(sp):
                def body(r, first, last):
                    for k in range(FB):
                        if not first:
                            sp.wait_ge(f_out[k], r * 16)
                            sp.sem_inc(passed2, 1)
                            sp.wait_ge(f_counted, r * FB + k - FB + 1)
                        sp.dma_start(fz[:, k, :], z_dram[bass.ds(r * FB + k, 1), :, :].rearrange(
                            "o p c -> (o p) c")).then_inc(z_in[k], 16)
                in_turns(sp, body)

            @b2.scalar
            def _(act):
                def body(r, first, last):
                    for k in range(FB):
                        act.wait_ge(z_in[k], (r + 1) * 16)
                        nc.scalar.activation(fz[:, k, :], fz[:, k, :], ACT.Sigmoid, bias=coef1[:, 1:2],
                                             scale=coef1[:, 0:1]).then_inc(f_ready, 1)
                in_turns(act, body)

            @b2.gpsimd
            def _(pool):
                def body(r, first, last):
                    for k in range(FB):
                        pool.wait_ge(f_ready, r * FB + k + 1)
                        pool.dma_start(f_dram[bass.ds(r * FB + k, 1), :, :].rearrange("o p c -> (o p) c"),
                                       fz[:, k, :]).then_inc(f_out[k], 16)
                in_turns(pool, body)
                for k in range(FB):
                    pool.wait_ge(f_out[k], LOOPS * 16)

            @b2.vector
            def _(dve):
                def body(r, first, last):
                    for k in range(FB):
                        dve.wait_ge(f_ready, r * FB + k + 1)
                        for q in range(SR):
                            s = (r * FB + k) * SR + q
                            v = fz[:, k, q * COLS:(q + 1) * COLS]
                            if not last or s < LAST:
                                m = nc.vector.bn_stats(stats[:, bass.ds(s, 1), :], v)
                            elif s == LAST:
                                even, odd = -(-LAST_TILES // 2) * P, LAST_TILES // 2 * P
                                nc.vector.bn_stats(stats[0:D, s, :], v[0:D, 0:even])
                                m = nc.vector.bn_stats(stats[D:P, s, :], v[D:P, 0:odd])
                        m.then_inc(f_counted, 1)
                in_turns(dve, body)

        coefficients("bn2", coef2, 2, 3)

        agg = sb("agg", [D, AGG_COLS])
        c3 = ExitStack()
        with c3:
            f = sb("f", [P, SR, RC], f32, c3)
            e = sb("e", [P, 2, RC], f32, c3)
            y = sb("y", [P, 2, RC], f32, c3)
            h = sb("h", [P, 2, RC], f32, c3)
            ht = sb("ht", [P, 2, TS, D], f32, c3)
            oh = sb("oh", [P, 2, TS, WIN], f32, c3)
            xrel = sb("xrel", [P, GT], f32, c3)
            ohx = sb("ohx", [P, GT, WIN], f32, c3)
            ps_h = [pb(f"ps_h{i}", [P, COLS], c3) for i in range(2)]
            ps_a = [pb(f"ps_a{i}", [D, 512], c3) for i in range(2)]
            ps_e = pb("ps_e", [D, 512], c3)
            f_in = [sem(f"f_in{i}", c3) for i in range(SR)]
            (exp_done, clamped, ln_done, y_done, sp_done, h_done, h_turned, ht_ready, oh_ready, summed,
             added, more_rel, more_oh, more_sum, passed3) = (sem(n, c3) for n in (
                 "exp_done", "clamped", "ln_done", "y_done", "sp_done", "h_done", "h_turned", "ht_ready",
                 "oh_ready", "summed", "added", "more_rel", "more_oh", "more_sum", "passed3"))
            STEPS = ROUNDS + 2
            b3 = c3.enter_context(nc.Block())

            def steps(eng, body):
                for i in range(SR):
                    body(i, i, i)
                with eng.Fori(SR, STEPS - 2 * SR + 1, SR) as i:
                    for q in range(SR):
                        body(i + q, q, SR)
                for i in range(STEPS - SR, STEPS):
                    body(i, i % SR, i)

            def has(i, low, back):
                return low >= back and (not isinstance(i, int) or i - back < ROUNDS)

            def tiles_of(i, q_super):
                s = (i - 2) * SR + q_super
                return real_tiles(s) if isinstance(s, int) else TS

            @b3.sync
            def _(sp):
                def body(i, q, low):
                    if not has(i, low, 0):
                        return
                    if low >= SR:
                        sp.wait_ge(h_done, i - SR + 1)
                    sp.dma_start(f[:, q, :], f_dram[bass.ds(i, 1), :, :].rearrange("o p c -> (o p) c")
                                 ).then_inc(f_in[q], 16)
                steps(sp, body)

            def arrivals(i, q):
                return (i // SR + 1) * 16 if isinstance(i, int) else (i - q) * (16 // SR) + 16

            @b3.scalar
            def _(act):
                def body(i, q, low):
                    if has(i, low, 0):
                        act.wait_ge(f_in[q], arrivals(i, q))
                        if low >= 2:
                            act.wait_ge(sp_done, i - 1)
                        nc.scalar.activation(e[:, q % 2, :], f[:, q, :], ACT.Exp, bias=coef2[:, 1:2],
                                             scale=coef2[:, 0:1]).then_inc(exp_done, 1)
                    if has(i, low, 2):
                        for k in range(SR):
                            s = (i - 2) * SR + k
                            if tiles_of(i, k) == 0:
                                continue
                            act.wait_ge(h_turned, s + 1)
                            if low > 2 or k >= 2:
                                act.wait_ge(summed, s - 1)
                            nc.scalar.copy(ht[:, k % 2, :, :].rearrange("p t d -> p (t d)"),
                                           ps_h[k % 2][:]).then_inc(ht_ready, 1)
                            if k == 1 and has(i, low, 1):
                                act.wait_ge(clamped, i)
                                nc.scalar.activation(e[:, (q + 1) % 2, :], e[:, (q + 1) % 2, :], ACT.Ln,
                                                     bias=1.0).then_inc(ln_done, 1)
                    elif has(i, low, 1):
                        act.wait_ge(clamped, i)
                        nc.scalar.activation(e[:, (q + 1) % 2, :], e[:, (q + 1) % 2, :], ACT.Ln,
                                             bias=1.0).then_inc(ln_done, 1)
                steps(act, body)

            @b3.gpsimd
            def _(pool):
                def body(i, q, low):
                    if has(i, low, 0):
                        pool.wait_ge(f_in[q], arrivals(i, q))
                        if low >= 2:
                            pool.wait_ge(h_done, i - 1)
                        pool.sem_inc(passed3, 1)
                        nc.gpsimd.tensor_scalar(y[:, q % 2, :], f[:, q, :], coef2[:, 0:1], coef2[:, 1:2],
                                                ALU.mult, ALU.add).then_inc(y_done, 1)
                    if has(i, low, 1):
                        pool.wait_ge(sp_done, i)
                        if low >= 3:
                            pool.wait_ge(h_turned, (i - 2) * SR)
                        o = (q + 1) % 2
                        nc.gpsimd.tensor_tensor(h[:, o, :], y[:, o, :], f[:, (q + 3) % SR, :],
                                                ALU.mult).then_inc(h_done, 1)
                steps(pool, body)

            @b3.vector
            def _(dve):
                nc.vector.memset(agg[:], 0.0).then_inc(added, 2)
                extra = dve.alloc_register("extra_windows")
                dve.reg_mov(extra, 0)

                def add_group(s, k, g, count):
                    w = dve.value_load(gmin_row[0:1, bass.ds(s * (TS // GT) + g, 1)], min_val=0, max_val=NODES - 1)
                    dve.wait_ge(added, count)
                    v = agg[:, bass.ds(w, WIN)]
                    nc.vector.tensor_tensor(v, v, ps_a[k % 2][:, g * WIN:(g + 1) * WIN], ALU.add).then_inc(added, 1)

                def more_windows(i, s, k, g):
                    gi = s * (TS // GT) + g
                    lo = dve.value_load(gmin_row[0:1, bass.ds(gi, 1)], min_val=0, max_val=NODES - 1)
                    hi = dve.value_load(gmax_row[0:1, bass.ds(gi, 1)], min_val=0, max_val=NODES - 1)
                    nc.vector.tensor_copy(xrel[:], dst_rel[:, bass.ds(gi * GT, GT)]).then_inc(more_rel, 1)
                    with dve.Fori(lo + WIN, hi + 1, WIN) as w:
                        dve.drain()
                        nc.vector.tensor_scalar(xrel[:], xrel[:], -float(WIN), None, ALU.add)
                        dve.drain()
                        nc.vector.tensor_tensor(
                            ohx[:], xrel[:].rearrange("p (t o) -> p t o", o=1).to_broadcast([P, GT, WIN]),
                            iota[:].rearrange("p (o w) -> p o w", o=1).to_broadcast([P, GT, WIN]),
                            ALU.is_equal).then_inc(more_oh, 1)
                        dve.reg_add(extra, extra, 1)
                        dve.wait_ge(more_sum, dve.snap(extra, min_val=1))
                        v = agg[:, bass.ds(w, WIN)]
                        nc.vector.tensor_tensor(v, v, ps_e[:, 0:WIN], ALU.add)
                        dve.drain()

                def body(i, q, low):
                    if has(i, low, 0):
                        dve.wait_ge(exp_done, i + 1)
                        nc.vector.tensor_scalar(e[:, q % 2, :], e[:, q % 2, :], EXP_MAX, None,
                                                ALU.min).then_inc(clamped, 1)
                    if has(i, low, 2):
                        wide = dve.value_load(span_row[0:1, bass.ds(i - 2, 1)], min_val=0, max_val=NODES)
                        for k in range(SR):
                            s = (i - 2) * SR + k
                            n = tiles_of(i, k)
                            if n:
                                if low > 2 or k >= 2:
                                    dve.wait_ge(summed, s - 1)
                                rel = dst_rel[:, bass.ds(s * TS, TS)]
                                nc.vector.tensor_tensor(
                                    oh[:, k % 2, :, :],
                                    rel.rearrange("p (t o) -> p t o", o=1).to_broadcast([P, TS, WIN]),
                                    iota[:].rearrange("p (o w) -> p o w", o=1).to_broadcast([P, TS, WIN]),
                                    ALU.is_equal).then_inc(oh_ready, 1)
                            if (low > 2 or k >= 1) and not (isinstance(s, int) and s > LAST + 1):
                                dve.wait_ge(summed, s)
                                for g in range(TS // GT):
                                    add_group(s - 1, (k - 1) % 2, g, (s - 1) * 2 + g + 2)
                            if n:
                                with dve.If(wide > WIN - 1):
                                    dve.wait_ge(summed, s + 1)
                                    for g in range(TS // GT):
                                        if g * GT < n:
                                            more_windows(i, s, k, g)
                    if has(i, low, 1):
                        dve.wait_ge(ln_done, i)
                        dve.wait_ge(y_done, i)
                        o = (q + 1) % 2
                        nc.vector.tensor_tensor(y[:, o, :], y[:, o, :], e[:, o, :], ALU.max).then_inc(sp_done, 1)
                steps(dve, body)

            @b3.tensor
            def _(pe):
                extra = pe.alloc_register("extra_windows_pe")
                pe.reg_mov(extra, 0)

                def body(i, q, low):
                    if not has(i, low, 2):
                        return
                    pe.wait_ge(h_done, i - 1)
                    wide = pe.value_load(span_row[0:1, bass.ds(i - 2, 1)], min_val=0, max_val=NODES)
                    for k in range(SR):
                        s = (i - 2) * SR + k
                        n = tiles_of(i, k)
                        if n == 0:
                            continue
                        if low > 2 or k >= 2:
                            pe.wait_ge(ht_ready, s - 1)
                        for j in range(TS // 2):
                            m = nc.tensor.transpose(ps_h[k % 2][:, j * P:(j + 1) * P],
                                                    h[:, q % 2, k * COLS + j * P:k * COLS + (j + 1) * P], ident[:])
                        m.then_inc(h_turned, 1)
                        pe.wait_ge(ht_ready, s + 1)
                        pe.wait_ge(oh_ready, s + 1)
                        if low > 2 or k >= 2:
                            pe.wait_ge(added, (s - 1) * 2 + 2)
                        for g in range(TS // GT):
                            for t in range(GT):
                                if g * GT + t < n:
                                    m = nc.tensor.matmul(ps_a[k % 2][:, g * WIN:(g + 1) * WIN],
                                                         ht[:, k % 2, g * GT + t, :], oh[:, k % 2, g * GT + t, :],
                                                         start=(t == 0), stop=(t == min(GT, n - g * GT) - 1))
                        m.then_inc(summed, 1)
                        with pe.If(wide > WIN - 1):
                            for g in range(TS // GT):
                                if g * GT >= n:
                                    continue
                                gi = s * (TS // GT) + g
                                lo = pe.value_load(gmin_row[0:1, bass.ds(gi, 1)], min_val=0, max_val=NODES - 1)
                                hi = pe.value_load(gmax_row[0:1, bass.ds(gi, 1)], min_val=0, max_val=NODES - 1)
                                with pe.Fori(lo + WIN, hi + 1, WIN):
                                    pe.reg_add(extra, extra, 1)
                                    pe.wait_ge(more_oh, pe.snap(extra, min_val=1))
                                    last_t = min(GT, n - g * GT) - 1
                                    for t in range(last_t + 1):
                                        m = nc.tensor.matmul(ps_e[:, 0:WIN], ht[:, k % 2, g * GT + t, :],
                                                             ohx[:, t, :], start=(t == 0), stop=(t == last_t))
                                    m.then_inc(more_sum, 1)
                                pe.nop()
                        pe.nop()
                steps(pe, body)

        c4 = ExitStack()
        with c4:
            x_s = sb("x_s", [P, NB, D], f32, c4)
            v = sb("v", [P, NB, D], f32, c4)
            w = sb("w", [P, NB, D], f32, c4)
            st = sb("st", [D, -(-NODES // 512), 6], f32, c4)
            k3 = sb("k3", [D, 8], f32, c4)
            ln = sb("ln", [P, 4, NB], f32, c4)
            KB = 8
            banks = [(b, min(KB, NB - b)) for b in range(0, NB, KB)]
            ps = [pb(f"ps_l{i}", [P, 512], c4) for i in range(2)]
            x_in, cleared, o_out, d, root, normed, turned, copied, sq = (
                sem(n, c4) for n in ("x_in", "cleared", "o_out", "d4", "root4", "normed", "turned4", "copied4", "sq4"))
            b4 = c4.enter_context(nc.Block())
            FULL = NODES // P

            @b4.sync
            def _(sp):
                sp.dma_start(x_s[:, 0:FULL, :], xn[0:FULL * P, :].rearrange("(b p) d -> p b d", p=P)).then_inc(x_in, 16)
                sp.wait_ge(cleared, 1)
                sp.dma_start(x_s[0:NODES - FULL * P, FULL, :], xn[FULL * P:NODES, :]).then_inc(x_in, 16)
                sp.wait_ge(normed, 2)
                sp.dma_start(out[0:FULL * P, :].rearrange("(b p) d -> p b d", p=P), v[:, 0:FULL, :]).then_inc(o_out, 16)
                sp.dma_start(out[FULL * P:NODES, :], v[0:NODES - FULL * P, FULL, :]).then_inc(o_out, 16)
                sp.wait_ge(o_out, 32)

            @b4.gpsimd
            def _(pool):
                nc.gpsimd.memset(x_s[64:P, FULL, :], 0.0).then_inc(cleared, 1)

            @b4.scalar
            def _(act):
                act.wait_ge(d, 3)
                nc.scalar.activation(k3[:, 3:4], k3[:, 2:3], ACT.Sqrt).then_inc(root, 1)
                act.wait_ge(sq, 1)
                nc.scalar.activation(w[:], v[:], ACT.Square).then_inc(sq, 1)
                act.wait_ge(sq, 4)
                nc.scalar.activation(ln[:, 2, :], ln[:, 1, :], ACT.Sqrt).then_inc(sq, 1)

            @b4.tensor
            def _(pe):
                pe.wait_ge(normed, 1)
                for i, (b0, n) in enumerate(banks):
                    if i >= 2:
                        pe.wait_ge(copied, i - 1)
                    for k in range(n):
                        m = nc.tensor.transpose(ps[i % 2][:, k * D:(k + 1) * D],
                                                agg[:, (b0 + k) * P:(b0 + k + 1) * P], ident[0:D, 0:D])
                    m.then_inc(turned, 1)

            @b4.vector
            def _(dve):
                n_done = [0]

                def then(i):
                    n_done[0] += 1
                    i.then_inc(d, 1)
                    dve.wait_ge(d, n_done[0])

                for j in range(-(-NODES // 512)):
                    m = nc.vector.bn_stats(st[:, j, :], agg[:, j * 512:min(NODES, (j + 1) * 512)])
                then(m)
                then(nc.vector.bn_aggr(k3[:, 0:2], st[:].rearrange("p s k -> p (s k)")))
                then(nc.vector.tensor_scalar(k3[:, 2:3], k3[:, 1:2], EPS, None, ALU.add))
                dve.wait_ge(root, 1)
                then(nc.vector.reciprocal(k3[:, 4:5], k3[:, 3:4]))
                then(nc.vector.tensor_tensor(k3[:, 5:6], k3[:, 4:5], par[0:D, 4:5], ALU.mult))
                then(nc.vector.tensor_tensor(k3[:, 6:7], k3[:, 0:1], k3[:, 5:6], ALU.mult))
                then(nc.vector.tensor_tensor(k3[:, 7:8], par[0:D, 5:6], k3[:, 6:7], ALU.subtract))
                nc.vector.tensor_scalar(agg[:], agg[:], k3[:, 5:6], k3[:, 7:8], ALU.mult, ALU.add).then_inc(normed, 1)
                dve.wait_ge(x_in, 32)
                for i, (b0, n) in enumerate(banks):
                    dve.wait_ge(turned, i + 1)
                    nc.vector.scalar_tensor_tensor(
                        w[:, b0:b0 + n, :].rearrange("p b d -> p (b d)"),
                        x_s[:, b0:b0 + n, :].rearrange("p b d -> p (b d)"), 2.0,
                        ps[i % 2][:, 0:n * D], ALU.mult, ALU.add).then_inc(copied, 1)
                dve.wait_ge(copied, len(banks))
                then(nc.vector.tensor_reduce(ln[:, 0, :], w[:], AX.X, ALU.add))
                then(nc.vector.tensor_scalar(ln[:, 1, :], ln[:, 0, :], 1.0 / D, None, ALU.mult))
                nc.vector.tensor_tensor(v[:], w[:], ln[:, 1, :].rearrange("p (b o) -> p b o", o=1).to_broadcast(
                    [P, NB, D]), ALU.subtract).then_inc(sq, 1)
                dve.wait_ge(sq, 2)
                nc.vector.tensor_reduce(ln[:, 0, :], w[:], AX.X, ALU.add).then_inc(sq, 1)
                dve.wait_ge(sq, 3)
                nc.vector.tensor_scalar(ln[:, 1, :], ln[:, 0, :], 1.0 / D, EPS, ALU.mult, ALU.add).then_inc(sq, 1)
                dve.wait_ge(sq, 5)
                then(nc.vector.reciprocal(ln[:, 3, :], ln[:, 2, :]))
                nc.vector.tensor_tensor(v[:], v[:], ln[:, 3, :].rearrange("p (b o) -> p b o", o=1).to_broadcast(
                    [P, NB, D]), ALU.mult).then_inc(normed, 1)


def kernel(x, src, dst, edge_attr_41, L0_gnn_W1, L0_gnn_b1, L0_gnn_W2, L0_gnn_b2, L0_gnn_g1, L0_gnn_bt1,
           L0_gnn_g2, L0_gnn_bt2, L0_gnn_g3, L0_gnn_bt3):
    import numpy as np
    import concourse.bacc as _bacc
    from concourse.bass_utils import run_bass_kernel_spmd as _run

    f = np.float32
    x, src, dst, ea, w1 = (np.asarray(a) for a in (x, src, dst, edge_attr_41, L0_gnn_W1))
    cols = [np.asarray(a) for a in (L0_gnn_g1, L0_gnn_bt1, L0_gnn_g2, L0_gnn_bt2, L0_gnn_g3, L0_gnn_bt3)]

    pad = PAD_EDGES - EDGES
    src_p = np.concatenate([src, np.zeros(pad, src.dtype)])
    dst_p = np.concatenate([dst, np.broadcast_to(dst[-1:], (pad,))])
    edge = np.zeros((SUPERS, KF - D, SUP), f)
    ea_p = np.concatenate([ea, np.zeros((pad, EF), f)]).reshape(SUPERS, SUP, EF)
    edge[:, 0:EF, :] = ea_p.transpose(0, 2, 1)
    edge[:, EF, :] = 1.0
    xT = np.zeros((D, PAD_NODES), f)
    xT[:, 0:NODES] = x.T
    w_edge = np.zeros((KF, D), f)
    w_edge[0:D] = w1[:, 0:D].T
    w_edge[D:D + EF] = w1[:, 2 * D:].T
    w_edge[D + EF] = np.asarray(L0_gnn_b1)
    even = (TILES // TS) * (TS // 2) * P + -(-LAST_TILES // 2) * P
    share = np.array([even / EDGES] * D + [(EDGES - even) / EDGES] * D, f).reshape(P, 1)
    k = np.arange(P)
    arrays = {
        "xT": xT, "xn": x, "src_cols": np.ascontiguousarray(src_p.reshape(SUPERS, TS, P).transpose(0, 2, 1)),
        "dst_cols": np.ascontiguousarray(dst_p.reshape(ALL_TILES, P).T),
        "dst_rows": dst_p.reshape(ROUNDS, SR * SUP), "edgeT": edge, "w_edge": w_edge,
        "w_dst": np.ascontiguousarray(w1[:, D:2 * D].T),
        "params": np.ascontiguousarray(np.stack([np.concatenate([c, c]) for c in cols], 1)),
        "wcol": share, "ident_in": np.eye(P, dtype=f), "fold_in": (k[:, None] % D == k[None, :] % D).astype(f),
        "nodecol_in": (k[:, None] + P * np.arange(NB)[None, :]).astype(f),
        "iota_in": np.broadcast_to(np.arange(WIN), (P, WIN)).astype(f),
    }
    nc = _bacc.Bacc("TRN2", target_bir_lowering=False, num_devices=1)
    args = [nc.dram_tensor(n, a.shape, mybir.dt.from_np(a.dtype), kind="ExternalInput").ap()
            for n, a in arrays.items()]
    args.append(nc.dram_tensor("out", (NODES, D), f32, kind="ExternalOutput").ap())
    gnn_kernel(nc, *args)
    r = _run(nc, [arrays], core_ids=[0])
    return r.results[0]["out"]
```

```python
import concourse.bass as bass
from concourse import mybir
from contextlib import ExitStack

NODES, EDGES, D, EF = 12500, 400000, 64, 41
P = 128
TS = 8
SUP = TS * P
SR = 4
COLS = SUP // 2
RC = SR * COLS
TILES = EDGES // P
ROUNDS = -(-EDGES // (SR * SUP))
SUPERS = ROUNDS * SR
ALL_TILES = SUPERS * TS
PAD_EDGES = SUPERS * SUP
LAST = TILES // TS
LAST_TILES = TILES - LAST * TS
NB = -(-NODES // P)
PAD_NODES = NB * P
GT = 4
GROUPS = ALL_TILES // GT
WIN = 64
AGG_COLS = PAD_NODES + 2 * WIN
XT_COLS = -(-NB // 16) * 8 * P
KF = 112
EPS = 1e-5

f32 = mybir.dt.float32
bf16 = mybir.dt.bfloat16
i32 = mybir.dt.int32
ALU = mybir.AluOpType
ACT = mybir.ActivationFunctionType
AX = mybir.AxisListType

EXP_MAX = 1e18
FB = 7
PARTS = 3


def real_tiles(s):
    return max(0, min(TS, TILES - s * TS))


def gnn_kernel(nc, xT, xn, src_cols, dst_cols, dst_rows, edgeT, w_edge, w_dst, params, wcol,
               ident_in, fold_in, nodecol_in, iota_in, out):
    ctx = ExitStack()
    with ctx:
        def sb(name, shape, dt=f32, c=ctx):
            return c.enter_context(nc.sbuf_tensor(name, shape, dt))

        def pb(name, shape, c, dt=f32):
            return c.enter_context(nc.psum_tensor(name, shape, dt))

        def sem(name, c=ctx):
            return c.enter_context(nc.semaphore(name))

        z_dram = nc.dram_tensor("z_dram", [ROUNDS, P, RC], f32).ap()
        f_dram = nc.dram_tensor("f_dram", [ROUNDS, P, RC], f32).ap()
        gmin_dram = nc.dram_tensor("gmin_dram", [ROUNDS, GROUPS // ROUNDS], i32).ap()
        gmax_dram = nc.dram_tensor("gmax_dram", [ROUNDS, GROUPS // ROUNDS], i32).ap()
        blk_dram = nc.dram_tensor("blk_dram", [ROUNDS, SR, 2], i32).ap()
        span_dram = nc.dram_tensor("span_dram", [ROUNDS, 1], i32).ap()

        ident = sb("ident", [P, P])
        fold = sb("fold", [P, P])
        par = sb("par", [P, 6])
        wc = sb("wc", [P, 1])
        gmin_row = sb("gmin_row", [1, GROUPS], i32)
        gmax_row = sb("gmax_row", [1, GROUPS], i32)
        span_row = sb("span_row", [1, ROUNDS], i32)
        dst_rel = sb("dst_rel", [P, ALL_TILES])
        coef1 = sb("coef1", [P, 2])
        coef2 = sb("coef2", [P, 2])
        stats = sb("stats", [P, LAST + 1, 6])
        iota = sb("iota", [P, WIN])

        c1 = ExitStack()
        with c1:
            blk_row = sb("blk_row", [1, 2 * SUPERS], i32, c1)
            w_e = sb("w_e", [KF, D], f32, c1)
            nodecol = sb("nodecol", [P, NB], f32, c1)
            pd = sb("pd", [P, NB, PARTS, D], bf16, c1)
            xT_s = sb("xT_s", [P, XT_COLS], f32, c1)
            w_d = sb("w_d", [P, D], f32, c1)
            dst_r = sb("dst_r", [ROUNDS, SR * SUP], i32, c1)
            dst_c = sb("dst_c", [P, ALL_TILES], i32, c1)
            gmin_b = sb("gmin_b", [P, GROUPS], i32, c1)
            gm = sb("gm", [ROUNDS, 2, GROUPS // ROUNDS], i32, c1)
            bl = sb("bl", [ROUNDS, SR, 2], i32, c1)
            bs = sb("bs", [ROUNDS, SR, 2], i32, c1)
            dif = sb("dif", [ROUNDS, GROUPS // ROUNDS], i32, c1)
            span = sb("span", [ROUNDS, 1], i32, c1)
            rest1 = sb("rest1", [P, 2, COLS], f32, c1)
            rest2 = sb("rest2", [P, 2, COLS], f32, c1)
            s_x, s_dr, s_dc, s_c, s_tab, s_row, s_gb, pd_mm, rng, first_part, less_one, second_part, less_two, \
                third_part, rel_done = (
                    sem(n, c1) for n in (
                        "s_x", "s_dr", "s_dc", "s_c", "s_tab", "s_row", "s_gb", "pd_mm", "rng", "first_part",
                        "less_one", "second_part", "less_two", "third_part", "rel_done"))
            src_ix = sb("src_ix", [P, SR, TS], i32, c1)
            G = sb("G", [P, SR, TS, D], f32, c1)
            xe = sb("xe", [KF, SR, SUP], f32, c1)
            dst_b = sb("dst_b", [P, SR, SUP], i32, c1)
            one_t = sb("one_t", [P, 2, SUP], bf16, c1)
            pd_cur = sb("pd_cur", [P, 2, PARTS, D], bf16, c1)
            zt = sb("zt", [P, SR, COLS], f32, c1)
            zero = sb("zero", [P, COLS], bf16, c1)
            ps_x = [pb(f"ps_x{i}", [D, SUP], c1) for i in range(2)]
            ps_z = [pb(f"ps_z{i}", [P, COLS], c1) for i in range(SR)]
            gathered = [sem(f"gathered{i}", c1) for i in range(SR)]
            src_in = [sem(f"src_in{i}", c1) for i in range(SR)]
            edge_in = [sem(f"edge_in{i}", c1) for i in range(SR)]
            dst_in = [sem(f"dst_in{i}", c1) for i in range(SR)]
            z_out = [sem(f"z_out{i}", c1) for i in range(SR)]
            zeroed, one_ready, one_used, g_turned, xe_ready, z_done, zt_ready, counted, passed = (
                sem(n, c1) for n in ("zeroed", "one_ready", "one_used", "g_turned", "xe_ready", "z_done",
                                     "zt_ready", "counted", "passed"))
            KB = COLS // D
            banks = [(b, min(KB, NB - b)) for b in range(0, NB, KB)]
            b1 = c1.enter_context(nc.Block())

            def rounds(eng, body):
                body(0, True, False)
                with eng.Fori(1, ROUNDS - 1) as r:
                    body(r, False, False)
                body(ROUNDS - 1, False, True)

            def super_blocks(eng, s):
                _, v = nc.values_load_multi_w_load_instructions(
                    blk_row[0:1, bass.ds(s * 2, 2)], engines=[eng.engine], min_val=0, max_val=NB - 1)
                return v

            @b1.gpsimd
            def _(pool):
                def body(r, first, last):
                    for q in range(SR):
                        if not first:
                            pool.wait_ge(g_turned, r * SR + q - SR + 1)
                        pool.wait_ge(src_in[q], (r + 1) * 16)
                        pool.sem_inc(passed, 1)
                        for t in range(TS):
                            nc.gpsimd.indirect_dma_start(
                                out=G[:, q, t, :], out_offset=None, in_=xn,
                                in_offset=bass.IndirectOffsetOnAxis(ap=src_ix[:, q, t:t + 1], axis=0),
                            ).then_inc(gathered[q], 16)
                rounds(pool, body)

            @b1.sync
            def _(sp):
                def load_src(r, q, first):
                    if not first:
                        sp.wait_ge(gathered[q], r * (16 * TS))
                    sp.dma_start(src_ix[:, q, :], src_cols[bass.ds(r * SR + q, 1), :, :].rearrange(
                        "o p t -> (o p) t")).then_inc(src_in[q], 16)

                for q in range(SR):
                    load_src(0, q, True)
                sp.dma_start(dst_r[:], dst_rows).then_inc(s_dr, 16)
                sp.dma_start(w_d[:], w_dst).then_inc(s_x, 16)
                sp.dma_start(xT_s[:], xT).then_inc(s_x, 16)
                for t, s in ((ident, ident_in), (w_e, w_edge), (nodecol, nodecol_in), (fold, fold_in),
                             (par, params), (wc, wcol), (iota, iota_in)):
                    sp.dma_start(t[:], s).then_inc(s_c, 16)
                sp.dma_start(dst_c[:], dst_cols).then_inc(s_dc, 16)
                sp.wait_ge(rng, 6)
                sp.dma_start(blk_dram, bs[:]).then_inc(s_tab, 16)
                sp.dma_start(gmin_dram, gm[:, 0, :]).then_inc(s_tab, 16)
                sp.dma_start(gmax_dram, gm[:, 1, :]).then_inc(s_tab, 16)
                sp.dma_start(span_dram, span[:]).then_inc(s_tab, 16)
                sp.wait_ge(s_tab, 64)
                for t, s, e in ((blk_row, blk_dram, "r s t -> (r s t)"), (gmin_row, gmin_dram, "r g -> (r g)"),
                                (gmax_row, gmax_dram, "r g -> (r g)"), (span_row, span_dram, "r o -> (r o)")):
                    sp.dma_start(t[:], s.rearrange(e)[None, :]).then_inc(s_row, 16)
                sp.dma_start(gmin_b[:], gmin_dram.rearrange("r g -> (r g)").partition_broadcast(P)
                             ).then_inc(s_gb, 16)

                def body(r, first, last):
                    for q in range(SR):
                        s = r * SR + q
                        if not first:
                            load_src(r, q, False)
                            sp.wait_ge(z_done, s - SR + 1)
                        sp.dma_start(xe[D:KF, q, :], edgeT[bass.ds(s, 1), :, :].rearrange("o k e -> (o k) e")
                                     ).then_inc(edge_in[q], 16)
                        if not first:
                            sp.wait_ge(counted, s - SR + 1)
                            sp.sem_inc(passed, 1)
                        sp.dma_start(dst_b[:, q, :],
                                     dst_rows[bass.ds(r, 1), q * SUP:(q + 1) * SUP].rearrange(
                                         "o e -> (o e)").partition_broadcast(P)).then_inc(dst_in[q], 16)
                rounds(sp, body)

            @b1.vector
            def _(dve):
                nc.vector.memset(zero[:], 0.0).then_inc(zeroed, 1)
                dve.wait_ge(s_dr, 16)
                by_group = dst_r[:].rearrange("r (g e) -> r g e", e=GT * P)
                nc.vector.tensor_reduce(gm[:, 0, :], by_group, AX.X, ALU.min).then_inc(rng, 1)
                nc.vector.tensor_reduce(gm[:, 1, :], by_group, AX.X, ALU.max).then_inc(rng, 1)
                dve.wait_ge(rng, 2)
                pairs = gm[:].rearrange("r m (s g) -> r m s g", g=TS // GT)
                nc.vector.tensor_tensor(bl[:, :, 0], pairs[:, 0, :, 0], pairs[:, 0, :, 1], ALU.min)
                nc.vector.tensor_tensor(bl[:, :, 1], pairs[:, 1, :, 0], pairs[:, 1, :, 1],
                                        ALU.max).then_inc(rng, 1)
                nc.vector.tensor_tensor(dif[:], gm[:, 1, :], gm[:, 0, :], ALU.subtract).then_inc(rng, 1)
                dve.wait_ge(rng, 4)
                nc.vector.tensor_single_scalar(bs[:], bl[:], 7, ALU.arith_shift_right).then_inc(rng, 1)
                nc.vector.tensor_reduce(span[:], dif[:], AX.X, ALU.max).then_inc(rng, 1)
                for i in range(len(banks) + 1):
                    if i < len(banks):
                        b0, n = banks[i]
                        dve.wait_ge(first_part, i + 1)
                        if i >= 2:
                            dve.wait_ge(second_part, i - 1)
                            dve.wait_ge(less_two, i - 1)
                        nc.vector.tensor_tensor(
                            rest1[:, i % 2, 0:n * D].rearrange("p (b d) -> p b d", d=D),
                            ps_z[i % SR][:, 0:n * D].rearrange("p (b d) -> p b d", d=D),
                            pd[:, b0:b0 + n, 0, :], ALU.subtract).then_inc(less_one, 1)
                    if i >= 1:
                        j = i - 1
                        b0, n = banks[j]
                        dve.wait_ge(second_part, j + 1)
                        if j >= 2:
                            dve.wait_ge(third_part, j - 1)
                        nc.vector.tensor_tensor(
                            rest2[:, j % 2, 0:n * D].rearrange("p (b d) -> p b d", d=D),
                            rest1[:, j % 2, 0:n * D].rearrange("p (b d) -> p b d", d=D),
                            pd[:, b0:b0 + n, 1, :], ALU.subtract).then_inc(less_two, 1)
                dve.wait_ge(third_part, len(banks))
                dve.wait_ge(s_row, 64)
                dve.wait_ge(s_c, 112)

                made = dve.alloc_register("marks_made")
                before = dve.alloc_register("marks_before")
                dve.reg_mov(made, 1)
                dve.reg_mov(before, 1)

                def marks(r, q):
                    s = r * SR + q
                    lo, hi = super_blocks(dve, s)
                    dve.wait_ge(dst_in[q], (r + 1) * 16)
                    dve.sem_inc(passed, 1)
                    dve.wait_ge(one_used, dve.snap(before, min_val=1))
                    dve.sem_inc(passed, 1)
                    dve.reg_mov(before, made)
                    with dve.Fori(lo, hi + 1) as b:
                        nc.vector.tensor_copy(pd_cur[:, q % 2, :, :],
                                              pd[:, bass.ds(b, 1), :, :].rearrange("p o k d -> p (o k) d"))
                        nc.vector.tensor_scalar(one_t[:, q % 2, :], dst_b[:, q, :],
                                                nodecol[:, bass.ds(b, 1)], None,
                                                ALU.is_equal).then_inc(one_ready, 1)
                        dve.reg_add(made, made, 1)
                        dve.wait_ge(one_used, dve.snap(made, min_val=1))

                def body(r, first, last):
                    for q in range(SR):
                        s = r * SR + q
                        if q + 1 < SR:
                            marks(r, q + 1)
                        elif not last:
                            marks(r + 1, 0)
                        dve.wait_ge(zt_ready, s + 1)
                        if not last or s < LAST:
                            nc.vector.bn_stats(stats[:, bass.ds(s, 1), :], zt[:, q, :]).then_inc(counted, 1)
                        elif s == LAST:
                            low, high = min(GT, LAST_TILES) * P, max(0, LAST_TILES - GT) * P
                            nc.vector.bn_stats(stats[0:D, s, :], zt[0:D, q, 0:low])
                            nc.vector.bn_stats(stats[D:P, s, :], zt[D:P, q, 0:high]).then_inc(counted, 1)
                marks(0, 0)
                dve.wait_ge(s_gb, 16)
                dve.wait_ge(s_dc, 16)
                nc.vector.tensor_tensor(dst_rel[:].rearrange("p (g t) -> p g t", t=GT),
                                        dst_c[:].rearrange("p (g t) -> p g t", t=GT),
                                        gmin_b[:].rearrange("p (g o) -> p g o", o=1).to_broadcast(
                                            [P, GROUPS, GT]), ALU.subtract).then_inc(rel_done, 1)
                rounds(dve, body)

            @b1.tensor
            def _(pe):
                pe.wait_ge(s_x, 32)
                for i, (b0, n) in enumerate(banks):
                    if i >= SR:
                        pe.wait_ge(less_one, i - SR + 1)
                    for k in range(n):
                        o, col = i % 2, i // 2 * KB + k
                        m = nc.tensor.matmul(ps_z[i % SR][:, k * D:(k + 1) * D],
                                             xT_s[o * D:(o + 1) * D, col * P:(col + 1) * P],
                                             w_d[o * D:(o + 1) * D, :], start=True, stop=True)
                    m.then_inc(pd_mm, 1)
                pe.wait_ge(less_one, len(banks))
                pe.wait_ge(zeroed, 1)
                pe.wait_ge(s_row, 64)
                pe.wait_ge(s_c, 112)
                pe.sem_inc(one_used, 1)
                seen = pe.alloc_register("marks_seen")
                pe.reg_mov(seen, 0)

                def from_dst(r, q, early):
                    s = r * SR + q
                    z = ps_z[q]
                    lo, hi = super_blocks(pe, s)
                    if not early:
                        pe.wait_ge(zt_ready, s - SR + 1)
                    for o in range(2):
                        nc.tensor.matmul(z[o * D:(o + 1) * D, :], zero[:, 0:D], zero[:], start=True, stop=False)
                    with pe.Fori(lo, hi + 1):
                        pe.reg_add(seen, seen, 1)
                        pe.wait_ge(one_ready, pe.snap(seen, min_val=1))
                        for part in range(PARTS):
                            for o in range(2):
                                m = nc.tensor.matmul(z[o * D:(o + 1) * D, :], pd_cur[:, q % 2, part, :],
                                                     one_t[:, q % 2, o * COLS:(o + 1) * COLS],
                                                     start=False, stop=False)
                        m.then_inc(one_used, 1)

                def body(r, first, last):
                    for q in range(SR):
                        s = r * SR + q
                        if not first or q >= 2:
                            pe.wait_ge(xe_ready, s - 1)
                        pe.wait_ge(gathered[q], (r + 1) * (16 * TS))
                        pe.sem_inc(passed, 1)
                        for t in range(TS):
                            m = nc.tensor.transpose(ps_x[q % 2][:, t * P:(t + 1) * P], G[:, q, t, :], ident[:])
                        m.then_inc(g_turned, 1)
                        if q + 1 < SR:
                            from_dst(r, q + 1, first)
                        elif not last:
                            from_dst(r + 1, 0, False)
                        pe.wait_ge(xe_ready, s + 1)
                        pe.wait_ge(edge_in[q], (r + 1) * 16)
                        for o in range(2):
                            m = nc.tensor.matmul(ps_z[q][o * D:(o + 1) * D, :], w_e[:],
                                                 xe[:, q, o * COLS:(o + 1) * COLS], start=False, stop=True)
                        m.then_inc(z_done, 1)
                from_dst(0, 0, True)
                rounds(pe, body)

            @b1.scalar
            def _(act):
                for i in range(len(banks) + 2):
                    if i < len(banks):
                        b0, n = banks[i]
                        act.wait_ge(pd_mm, i + 1)
                        nc.scalar.copy(pd[:, b0:b0 + n, 0, :],
                                       ps_z[i % SR][:, 0:n * D].rearrange("p (b d) -> p b d", d=D)
                                       ).then_inc(first_part, 1)
                    if 1 <= i <= len(banks):
                        j = i - 1
                        b0, n = banks[j]
                        act.wait_ge(less_one, j + 1)
                        nc.scalar.copy(pd[:, b0:b0 + n, 1, :],
                                       rest1[:, j % 2, 0:n * D].rearrange("p (b d) -> p b d", d=D)
                                       ).then_inc(second_part, 1)
                    if i >= 2:
                        j = i - 2
                        b0, n = banks[j]
                        act.wait_ge(less_two, j + 1)
                        nc.scalar.copy(pd[:, b0:b0 + n, 2, :],
                                       rest2[:, j % 2, 0:n * D].rearrange("p (b d) -> p b d", d=D)
                                       ).then_inc(third_part, 1)

                def body(r, first, last):
                    for q in range(SR):
                        s = r * SR + q
                        act.wait_ge(g_turned, s + 1)
                        if not first:
                            act.wait_ge(z_done, s - SR + 1)
                        nc.scalar.copy(xe[0:D, q, :], ps_x[q % 2][:]).then_inc(xe_ready, 1)
                        act.wait_ge(z_done, s + 1)
                        if not first:
                            act.wait_ge(z_out[q], r * 16)
                            act.wait_ge(counted, s - SR + 1)
                        nc.scalar.copy(zt[:, q, :], ps_z[q][:]).then_inc(zt_ready, 1)
                        act.wait_ge(zt_ready, s + 1)
                        act.dma_start(z_dram[bass.ds(r, 1), :, q * COLS:(q + 1) * COLS].rearrange(
                            "o p c -> (o p) c"), zt[:, q, :]).then_inc(z_out[q], 16)
                rounds(act, body)
                for q in range(SR):
                    act.wait_ge(z_out[q], ROUNDS * 16)

        def coefficients(name, coef, gamma, beta):
            c = ExitStack()
            with c:
                v = sb(name + "_v", [P, 12], f32, c)
                ps = pb(name + "_ps", [P, 2], c)
                done, summed, rooted = sem(name + "_done", c), sem(name + "_summed", c), sem(name + "_rooted", c)
                blk = c.enter_context(nc.Block())

                @blk.vector
                def _(dve):
                    n = [0]

                    def then(i):
                        n[0] += 1
                        i.then_inc(done, 1)
                        dve.wait_ge(done, n[0])

                    nc.vector.memset(v[:, 2:12], 0.0)
                    then(nc.vector.bn_aggr(v[:, 0:2], stats[:].rearrange("p s k -> p (s k)")))
                    then(nc.vector.tensor_tensor(v[:, 2:3], v[:, 0:1], wc[:], ALU.mult))
                    dve.wait_ge(summed, 1)
                    then(nc.vector.tensor_copy(v[:, 3:4], ps[:, 0:1]))
                    then(nc.vector.tensor_tensor(v[:, 4:5], v[:, 0:1], v[:, 3:4], ALU.subtract))
                    then(nc.vector.tensor_tensor(v[:, 5:6], v[:, 4:5], v[:, 4:5], ALU.mult))
                    then(nc.vector.tensor_tensor(v[:, 6:7], v[:, 5:6], v[:, 1:2], ALU.add))
                    then(nc.vector.tensor_tensor(v[:, 7:8], v[:, 6:7], wc[:], ALU.mult))
                    dve.wait_ge(summed, 2)
                    then(nc.vector.tensor_scalar(v[:, 8:9], ps[:, 1:2], EPS, None, ALU.add))
                    dve.wait_ge(rooted, 1)
                    then(nc.vector.reciprocal(v[:, 10:11], v[:, 9:10]))
                    then(nc.vector.tensor_tensor(coef[:, 0:1], v[:, 10:11], par[:, gamma:gamma + 1], ALU.mult))
                    then(nc.vector.tensor_tensor(v[:, 11:12], v[:, 3:4], coef[:, 0:1], ALU.mult))
                    then(nc.vector.tensor_tensor(coef[:, 1:2], par[:, beta:beta + 1], v[:, 11:12], ALU.subtract))

                @blk.tensor
                def _(pe):
                    pe.wait_ge(done, 2)
                    nc.tensor.matmul(ps[:, 0:1], fold[:], v[:, 2:3], start=True, stop=True).then_inc(summed, 1)
                    pe.wait_ge(done, 7)
                    nc.tensor.matmul(ps[:, 1:2], fold[:], v[:, 7:8], start=True, stop=True).then_inc(summed, 1)

                @blk.scalar
                def _(act):
                    act.wait_ge(done, 8)
                    nc.scalar.activation(v[:, 9:10], v[:, 8:9], ACT.Sqrt).then_inc(rooted, 1)

        coefficients("bn1", coef1, 0, 1)

        c2 = ExitStack()
        with c2:
            fz = sb("fz", [P, FB, RC], f32, c2)
            z_in = [sem(f"z_in{i}", c2) for i in range(FB)]
            f_out = [sem(f"f_out{i}", c2) for i in range(FB)]
            f_ready, f_counted, passed2 = sem("f_ready", c2), sem("f_counted", c2), sem("passed2", c2)
            LOOPS = ROUNDS // FB
            AHEAD = 4
            b2 = c2.enter_context(nc.Block())

            def in_turns(eng, body):
                body(0, True, False)
                with eng.Fori(1, LOOPS - 1) as r:
                    body(r, False, False)
                body(LOOPS - 1, False, True)

            @b2.sync
            def _(sp):
                def body(r, first, last):
                    for k in range(FB):
                        if not first:
                            sp.wait_ge(f_out[k], r * 16)
                            sp.sem_inc(passed2, 1)
                            sp.wait_ge(f_counted, r * FB + k - FB + 1)
                        sp.dma_start(fz[:, k, :], z_dram[bass.ds(r * FB + k, 1), :, :].rearrange(
                            "o p c -> (o p) c")).then_inc(z_in[k], 16)
                in_turns(sp, body)

            @b2.scalar
            def _(act):
                def body(r, first, last):
                    for k in range(FB):
                        act.wait_ge(z_in[k], (r + 1) * 16)
                        nc.scalar.activation(fz[:, k, :], fz[:, k, :], ACT.Sigmoid, bias=coef1[:, 1:2],
                                             scale=coef1[:, 0:1]).then_inc(f_ready, 1)
                in_turns(act, body)

            @b2.gpsimd
            def _(pool):
                def body(r, first, last):
                    for k in range(FB):
                        pool.wait_ge(f_ready, r * FB + k + 1)
                        pool.dma_start(f_dram[bass.ds(r * FB + k, 1), :, :].rearrange("o p c -> (o p) c"),
                                       fz[:, k, :]).then_inc(f_out[k], 16)
                in_turns(pool, body)
                for k in range(FB):
                    pool.wait_ge(f_out[k], LOOPS * 16)

            @b2.vector
            def _(dve):
                def body(r, first, last):
                    for k in range(FB):
                        dve.wait_ge(f_ready, r * FB + k + 1)
                        for q in range(SR):
                            s = (r * FB + k) * SR + q
                            v = fz[:, k, q * COLS:(q + 1) * COLS]
                            if not last or s < LAST:
                                m = nc.vector.bn_stats(stats[:, bass.ds(s, 1), :], v)
                            elif s == LAST:
                                low, high = min(GT, LAST_TILES) * P, max(0, LAST_TILES - GT) * P
                                nc.vector.bn_stats(stats[0:D, s, :], v[0:D, 0:low])
                                m = nc.vector.bn_stats(stats[D:P, s, :], v[D:P, 0:high])
                        m.then_inc(f_counted, 1)
                in_turns(dve, body)

        coefficients("bn2", coef2, 2, 3)

        agg = sb("agg", [P, AGG_COLS])
        c3 = ExitStack()
        with c3:
            f = sb("f", [P, SR, RC], f32, c3)
            e = sb("e", [P, SR, RC], f32, c3)
            y = sb("y", [P, 2, RC], f32, c3)
            h = sb("h", [P, 2, RC], f32, c3)
            ht = sb("ht", [P, 2, 2 * GT, 2, D], f32, c3)
            oh = sb("oh", [P, 2, 2 * TS, WIN], f32, c3)
            xrel = sb("xrel", [P, GT], f32, c3)
            ohx = sb("ohx", [P, GT, WIN], f32, c3)
            ps_h = [pb(f"ps_h{i}", [P, 2 * COLS], c3) for i in range(2)]
            ps_a = [pb(f"ps_a{i}", [P, COLS], c3) for i in range(2)]
            ps_e = pb("ps_e", [P, COLS], c3)
            f_in = [sem(f"f_in{i}", c3) for i in range(SR)]
            (exp_done, clamped, ln_done, y_done, sp_done, h_done, h_turned, ht_ready, oh_ready, summed,
             added, more_oh, more_sum, passed3) = (sem(n, c3) for n in (
                 "exp_done", "clamped", "ln_done", "y_done", "sp_done", "h_done", "h_turned", "ht_ready",
                 "oh_ready", "summed", "added", "more_oh", "more_sum", "passed3"))
            UNITS = -(-TILES // (2 * TS))
            UG = 2 * TS // GT
            STEPS = ROUNDS + 4
            LOOP_END = ROUNDS - ROUNDS % SR
            b3 = c3.enter_context(nc.Block())

            def steps(eng, body):
                for i in range(SR):
                    body(i, i, i)
                with eng.Fori(SR, LOOP_END - SR + 1, SR) as i:
                    for q in range(SR):
                        body(i + q, q, SR + q)
                for i in range(LOOP_END, STEPS):
                    body(i, i % SR, i)

            def has(i, low, back):
                return low >= back and (not isinstance(i, int) or i - back < ROUNDS)

            def units(i, low):
                return [(i - 3, half, low - 3) for half in range(2)]

            def before(r, half, low):
                return (r, 0, low) if half else (r - 1, 1, low - 1)

            def is_unit(r, half, low):
                return low >= 0 and (not isinstance(r, int) or r * 2 + half < UNITS)

            def tiles_in(u, g):
                return max(0, min(GT, TILES - (u * UG + g) * GT)) if isinstance(u, int) else GT

            def arrivals(i, q):
                return (i // SR + 1) * 16 if isinstance(i, int) else (i - q) * (16 // SR) + 16

            def group_range(eng, g):
                return (eng.value_load(gmin_row[0:1, bass.ds(g, 1)], min_val=0, max_val=NODES - 1),
                        eng.value_load(gmax_row[0:1, bass.ds(g, 1)], min_val=0, max_val=NODES - 1))

            def is_wide(eng, r):
                return eng.value_load(span_row[0:1, bass.ds(r, 1)], min_val=0, max_val=NODES)

            @b3.sync
            def _(sp):
                def body(i, q, low):
                    if not has(i, low, 0):
                        return
                    if low >= SR:
                        sp.wait_ge(h_done, i - SR + 1)
                    sp.dma_start(f[:, q, :], f_dram[bass.ds(i, 1), :, :].rearrange("o p c -> (o p) c")
                                 ).then_inc(f_in[q], 16)
                steps(sp, body)

            @b3.scalar
            def _(act):
                nc.scalar.preload_act_table_set("natural_log_exp_and_others")

                def turn_out(r, half, low):
                    if is_unit(r, half, low):
                        act.wait_ge(h_turned, r * 2 + half + 1)
                        nc.scalar.copy(ht[:, half, :, :, :].rearrange("p t o d -> p (t o d)"),
                                       ps_h[half][:]).then_inc(ht_ready, 1)

                def body(i, q, low):
                    turns = units(i, low)
                    if has(i, low, 0):
                        act.wait_ge(f_in[q], arrivals(i, q))
                        if low >= SR:
                            act.wait_ge(sp_done, i - SR + 1)
                        nc.scalar.activation(e[:, q, :], f[:, q, :], ACT.Exp, bias=coef2[:, 1:2],
                                             scale=coef2[:, 0:1]).then_inc(exp_done, 1)
                    turn_out(*turns[0])
                    if has(i, low, 1):
                        o = (q + 3) % SR
                        act.wait_ge(clamped, i)
                        nc.scalar.activation(e[:, o, :], e[:, o, :], ACT.Ln, bias=1.0).then_inc(ln_done, 1)
                    turn_out(*turns[1])
                steps(act, body)

            @b3.gpsimd
            def _(pool):
                def body(i, q, low):
                    if has(i, low, 1):
                        pool.wait_ge(f_in[(q + 3) % SR], arrivals(i - 1, (q + 3) % SR)
                                     if isinstance(i, int) else
                                     (arrivals(i, q) if q else arrivals(i, q) - 16))
                        if low >= 3:
                            pool.wait_ge(h_done, i - 2)
                        pool.sem_inc(passed3, 1)
                        nc.gpsimd.tensor_scalar(y[:, (q + 1) % 2, :], f[:, (q + 3) % SR, :], coef2[:, 0:1],
                                                coef2[:, 1:2], ALU.mult, ALU.add).then_inc(y_done, 1)
                    if has(i, low, 2):
                        pool.wait_ge(sp_done, i - 1)
                        if low >= 4:
                            pool.wait_ge(h_turned, (i - 3) * 2)
                        nc.gpsimd.tensor_tensor(h[:, q % 2, :], y[:, q % 2, :], f[:, (q + 2) % SR, :],
                                                ALU.mult).then_inc(h_done, 1)
                steps(pool, body)

            @b3.vector
            def _(dve):
                nc.vector.memset(agg[:], 0.0).then_inc(added, 2)
                extra = dve.alloc_register("extra_windows")
                dve.reg_mov(extra, 0)

                def mark(r, half, low):
                    if not is_unit(r, half, low):
                        return
                    u = r * 2 + half
                    if low >= 1:
                        dve.wait_ge(summed, u - 1)
                    rel = dst_rel[:, bass.ds(u * (2 * TS), 2 * TS)]
                    nc.vector.tensor_tensor(
                        oh[:, half, :, :],
                        rel.rearrange("p (t o) -> p t o", o=1).to_broadcast([P, 2 * TS, WIN]),
                        iota[:].rearrange("p (o w) -> p o w", o=1).to_broadcast([P, 2 * TS, WIN]),
                        ALU.is_equal).then_inc(oh_ready, 1)

                def add(r, half, low):
                    if not is_unit(r, half, low):
                        return
                    u = r * 2 + half
                    _, at = nc.values_load_multi_w_load_instructions(
                        gmin_row[0:1, bass.ds(u * UG, UG)], engines=[dve.engine], min_val=0, max_val=NODES - 1)
                    dve.wait_ge(summed, u + 1)
                    for g in range(UG):
                        rows = slice(g % 2 * D, g % 2 * D + D)
                        v = agg[rows, bass.ds(at[g], WIN)]
                        if tiles_in(u, g):
                            dve.wait_ge(added, u * UG + g + 1)
                            nc.vector.tensor_tensor(v, v, ps_a[half][rows, g // 2 * WIN:(g // 2 + 1) * WIN],
                                                    ALU.add).then_inc(added, 1)
                    more_windows(r, u)

                def more_windows(r, u):
                    with dve.If(is_wide(dve, r) > WIN - 1):
                        for g in range(UG):
                            if not tiles_in(u, g):
                                continue
                            rows = slice(g % 2 * D, g % 2 * D + D)
                            lo, hi = group_range(dve, u * UG + g)
                            dve.drain()
                            nc.vector.tensor_copy(xrel[:], dst_rel[:, bass.ds((u * UG + g) * GT, GT)])
                            with dve.Fori(lo + WIN, hi + 1, WIN) as w:
                                dve.drain()
                                nc.vector.tensor_scalar(xrel[:], xrel[:], -float(WIN), None, ALU.add)
                                dve.drain()
                                nc.vector.tensor_tensor(
                                    ohx[:], xrel[:].rearrange("p (t o) -> p t o", o=1).to_broadcast([P, GT, WIN]),
                                    iota[:].rearrange("p (o w) -> p o w", o=1).to_broadcast([P, GT, WIN]),
                                    ALU.is_equal).then_inc(more_oh, 1)
                                dve.reg_add(extra, extra, 1)
                                dve.wait_ge(more_sum, dve.snap(extra, min_val=1))
                                v = agg[rows, bass.ds(w, WIN)]
                                nc.vector.tensor_tensor(v, v, ps_e[rows, 0:WIN], ALU.add)
                        dve.drain()

                def body(i, q, low):
                    turns = units(i, low)
                    mark(*turns[0])
                    add(*before(*turns[0]))
                    if has(i, low, 2):
                        o = (q + 2) % SR
                        dve.wait_ge(ln_done, i - 1)
                        dve.wait_ge(y_done, i - 1)
                        nc.vector.tensor_tensor(y[:, q % 2, :], y[:, q % 2, :], e[:, o, :],
                                                ALU.max).then_inc(sp_done, 1)
                    mark(*turns[1])
                    add(*before(*turns[1]))
                    if has(i, low, 0):
                        dve.wait_ge(exp_done, i + 1)
                        nc.vector.tensor_scalar(e[:, q, :], e[:, q, :], EXP_MAX, None,
                                                ALU.min).then_inc(clamped, 1)
                steps(dve, body)

            @b3.tensor
            def _(pe):
                extra = pe.alloc_register("extra_windows_pe")
                pe.reg_mov(extra, 0)

                def turn(r, half, low):
                    if not is_unit(r, half, low):
                        return
                    if half == 0:
                        pe.wait_ge(h_done, r + 1)
                    if low >= 1:
                        pe.wait_ge(ht_ready, r * 2 + half - 1)
                    for j in range(2 * GT):
                        col = half * 2 * COLS + j * P
                        m = nc.tensor.transpose(ps_h[half][:, j * P:(j + 1) * P],
                                                h[:, low % 2, col:col + P], ident[:])
                    m.then_inc(h_turned, 1)

                def sum_up(r, half, low):
                    if not is_unit(r, half, low):
                        return
                    u = r * 2 + half
                    pe.wait_ge(ht_ready, u + 1)
                    pe.wait_ge(oh_ready, u + 1)
                    if low >= 1:
                        pe.wait_ge(added, (u - 1) * UG + 2)
                    for g in range(UG):
                        n = tiles_in(u, g)
                        rows = slice(g % 2 * D, g % 2 * D + D)
                        for t in range(n):
                            m = nc.tensor.matmul(ps_a[half][rows, g // 2 * WIN:(g // 2 + 1) * WIN],
                                                 ht[:, half, g // 2 * GT + t, g % 2, :],
                                                 oh[:, half, g * GT + t, :], start=(t == 0), stop=(t == n - 1))
                    m.then_inc(summed, 1)
                    with pe.If(is_wide(pe, r) > WIN - 1):
                        for g in range(UG):
                            n = tiles_in(u, g)
                            if not n:
                                continue
                            rows = slice(g % 2 * D, g % 2 * D + D)
                            lo, hi = group_range(pe, u * UG + g)
                            with pe.Fori(lo + WIN, hi + 1, WIN):
                                pe.reg_add(extra, extra, 1)
                                pe.wait_ge(more_oh, pe.snap(extra, min_val=1))
                                for t in range(n):
                                    m = nc.tensor.matmul(ps_e[rows, 0:WIN],
                                                         ht[:, half, g // 2 * GT + t, g % 2, :],
                                                         ohx[:, t, :], start=(t == 0), stop=(t == n - 1))
                                m.then_inc(more_sum, 1)
                        pe.nop()

                def body(i, q, low):
                    for unit in units(i, low):
                        turn(*unit)
                        sum_up(*before(*unit))
                steps(pe, body)

        c4 = ExitStack()
        with c4:
            x_s = sb("x_s", [P, NB, D], f32, c4)
            v = sb("v", [P, NB, D], f32, c4)
            w = sb("w", [P, NB, D], f32, c4)
            NS = -(-NODES // COLS)
            st = sb("st", [P, NS, 6], f32, c4)
            k3 = sb("k3", [P, 8], f32, c4)
            w_scale = sb("w_scale", [P, D], f32, c4)
            w_shift = sb("w_shift", [P, D], f32, c4)
            ones = sb("ones", [P, P], f32, c4)
            ln = sb("ln", [P, 5, NB], f32, c4)
            KB = COLS // D
            banks = [(b, min(KB, NB - b)) for b in range(0, NB, KB)]
            pieces = [(0, 4), (4, 8), (8, 11), (11, len(banks))]
            spans = [(banks[a][0], banks[b - 1][0] + banks[b - 1][1]) for a, b in pieces]
            ps_s = [pb(f"ps_s{i}", [P, COLS], c4) for i in range(2)]
            ps_n = [pb(f"ps_n{i}", [P, COLS], c4) for i in range(4)]
            (x_in, cleared, o_out, folded, read, d, root, scaled, turned, copied, centred, squared, spread,
             rooted, inverted, normed) = (
                sem(n, c4) for n in ("x_in", "cleared", "o_out", "folded", "read4", "d4", "root4", "scaled",
                                     "turned4", "copied4", "centred", "squared", "spread", "rooted",
                                     "inverted", "normed"))
            b4 = c4.enter_context(nc.Block())
            FULL = NODES // P

            def wide(a, b0, b1):
                return a[:, b0:b1].rearrange("p (b o) -> p b o", o=1).to_broadcast([P, b1 - b0, D])

            @b4.sync
            def _(sp):
                sp.dma_start(x_s[:, 0:FULL, :], xn[0:FULL * P, :].rearrange("(b p) d -> p b d", p=P)).then_inc(x_in, 16)
                sp.wait_ge(cleared, 1)
                sp.dma_start(x_s[0:NODES - FULL * P, FULL, :], xn[FULL * P:NODES, :]).then_inc(x_in, 16)
                for i, (b0, b1) in enumerate(spans):
                    sp.wait_ge(normed, i + 1)
                    e = min(b1, FULL)
                    sp.dma_start(out[b0 * P:e * P, :].rearrange("(b p) d -> p b d", p=P),
                                 v[:, b0:e, :]).then_inc(o_out, 16)
                sp.dma_start(out[FULL * P:NODES, :], v[0:NODES - FULL * P, FULL, :]).then_inc(o_out, 16)
                sp.wait_ge(o_out, 16 * len(spans) + 16)

            @b4.gpsimd
            def _(pool):
                nc.gpsimd.memset(x_s[64:P, FULL, :], 0.0).then_inc(cleared, 1)
                pool.wait_ge(cleared, 1)
                nc.gpsimd.memset(ones[:], 1.0).then_inc(cleared, 1)
                for i, (b0, b1) in enumerate(spans):
                    pool.wait_ge(inverted, i + 1)
                    nc.gpsimd.tensor_tensor(v[:, b0:b1, :], v[:, b0:b1, :], wide(ln[:, 4, :], b0, b1),
                                            ALU.mult).then_inc(normed, 1)

            @b4.scalar
            def _(act):
                act.wait_ge(d, 3)
                nc.scalar.activation(k3[:, 3:4], k3[:, 2:3], ACT.Sqrt).then_inc(root, 1)
                for i, (b0, b1) in enumerate(spans):
                    act.wait_ge(centred, i + 1)
                    nc.scalar.activation(w[:, b0:b1, :], v[:, b0:b1, :], ACT.Square).then_inc(squared, 1)
                    act.wait_ge(spread, 2 * i + 2)
                    nc.scalar.activation(ln[:, 3, b0:b1], ln[:, 2, b0:b1], ACT.Sqrt).then_inc(rooted, 1)

            @b4.tensor
            def _(pe):
                for j in range(NS):
                    if j >= 2:
                        pe.wait_ge(read, j - 1)
                    n = min(COLS, NODES - j * COLS)
                    nc.tensor.matmul(ps_s[j % 2][:, 0:n], fold[:], agg[:, j * COLS:j * COLS + n],
                                     start=True, stop=True).then_inc(folded, 1)
                pe.wait_ge(scaled, 2)
                pe.wait_ge(cleared, 2)
                for i, (b0, n) in enumerate(banks):
                    if i >= 4:
                        pe.wait_ge(copied, i - 3)
                    for k in range(n):
                        o = ps_n[i % 4][:, k * D:(k + 1) * D]
                        nc.tensor.matmul(o, agg[:, (b0 + k) * P:(b0 + k + 1) * P], w_scale[:],
                                         start=True, stop=False)
                        m = nc.tensor.matmul(o, ones[:], w_shift[:], start=False, stop=True)
                    m.then_inc(turned, 1)

            @b4.vector
            def _(dve):
                n_done = [0]

                def then(i):
                    n_done[0] += 1
                    i.then_inc(d, 1)
                    dve.wait_ge(d, n_done[0])

                for j in range(NS):
                    dve.wait_ge(folded, j + 1)
                    nc.vector.bn_stats(st[:, j, :], ps_s[j % 2][:, 0:min(COLS, NODES - j * COLS)]).then_inc(read, 1)
                dve.wait_ge(read, NS)
                then(nc.vector.bn_aggr(k3[:, 0:2], st[:].rearrange("p s k -> p (s k)")))
                then(nc.vector.tensor_scalar(k3[:, 2:3], k3[:, 1:2], EPS, None, ALU.add))
                then(nc.vector.memset(k3[:, 7:8], 1.0 / 2))
                dve.wait_ge(root, 1)
                then(nc.vector.reciprocal(k3[:, 4:5], k3[:, 3:4]))
                then(nc.vector.tensor_tensor(k3[:, 5:6], k3[:, 4:5], par[:, 4:5], ALU.mult))
                nc.vector.tensor_scalar(w_scale[:], fold[:, 0:D], k3[:, 5:6], None, ALU.mult).then_inc(scaled, 1)
                then(nc.vector.tensor_tensor(k3[:, 6:7], k3[:, 0:1], k3[:, 5:6], ALU.mult))
                then(nc.vector.tensor_tensor(k3[:, 6:7], par[:, 5:6], k3[:, 6:7], ALU.subtract))
                nc.vector.tensor_scalar(w_shift[:], fold[:, 0:D], k3[:, 6:7], k3[:, 7:8],
                                        ALU.mult, ALU.mult).then_inc(scaled, 1)
                dve.wait_ge(x_in, 32)

                def residual(i):
                    b0, n = banks[i]
                    dve.wait_ge(turned, i + 1)
                    nc.vector.scalar_tensor_tensor(
                        w[:, b0:b0 + n, :].rearrange("p b d -> p (b d)"),
                        x_s[:, b0:b0 + n, :].rearrange("p b d -> p (b d)"), 2.0,
                        ps_n[i % 4][:, 0:n * D], ALU.mult, ALU.add).then_inc(copied, 1)

                def centre(p):
                    b0, b1 = spans[p]
                    dve.wait_ge(copied, pieces[p][1])
                    then(nc.vector.tensor_reduce(ln[:, 0, b0:b1], w[:, b0:b1, :], AX.X, ALU.add))
                    then(nc.vector.tensor_scalar(ln[:, 1, b0:b1], ln[:, 0, b0:b1], 1.0 / D, None, ALU.mult))
                    nc.vector.tensor_tensor(v[:, b0:b1, :], w[:, b0:b1, :], wide(ln[:, 1, :], b0, b1),
                                            ALU.subtract).then_inc(centred, 1)

                def variance(p):
                    b0, b1 = spans[p]
                    dve.wait_ge(squared, p + 1)
                    nc.vector.tensor_reduce(ln[:, 0, b0:b1], w[:, b0:b1, :], AX.X, ALU.add).then_inc(spread, 1)
                    dve.wait_ge(spread, 2 * p + 1)
                    nc.vector.tensor_scalar(ln[:, 2, b0:b1], ln[:, 0, b0:b1], 1.0 / D, EPS,
                                            ALU.mult, ALU.add).then_inc(spread, 1)

                def invert(p):
                    b0, b1 = spans[p]
                    dve.wait_ge(rooted, p + 1)
                    nc.vector.reciprocal(ln[:, 4, b0:b1], ln[:, 3, b0:b1]).then_inc(inverted, 1)

                for p in range(len(pieces) + 1):
                    if p < len(pieces):
                        for i in range(*pieces[p]):
                            residual(i)
                    if p >= 1:
                        variance(p - 1)
                    if p < len(pieces):
                        centre(p)
                    if p >= 1:
                        invert(p - 1)


def kernel(x, src, dst, edge_attr_41, L0_gnn_W1, L0_gnn_b1, L0_gnn_W2, L0_gnn_b2, L0_gnn_g1, L0_gnn_bt1,
           L0_gnn_g2, L0_gnn_bt2, L0_gnn_g3, L0_gnn_bt3):
    import numpy as np
    import concourse.bacc as _bacc
    from concourse.bass_utils import run_bass_kernel_spmd as _run

    f = np.float32
    x, src, dst, ea, w1 = (np.asarray(a) for a in (x, src, dst, edge_attr_41, L0_gnn_W1))
    cols = [np.asarray(a) for a in (L0_gnn_g1, L0_gnn_bt1, L0_gnn_g2, L0_gnn_bt2, L0_gnn_g3, L0_gnn_bt3)]

    pad = PAD_EDGES - EDGES
    src_p = np.concatenate([src, np.zeros(pad, src.dtype)])
    dst_p = np.concatenate([dst, np.broadcast_to(dst[-1:], (pad,))])
    edge = np.zeros((SUPERS, KF - D, SUP), f)
    ea_p = np.concatenate([ea, np.zeros((pad, EF), f)]).reshape(SUPERS, SUP, EF)
    edge[:, 0:EF, :] = ea_p.transpose(0, 2, 1)
    edge[:, EF, :] = 1.0
    xT = np.zeros((D, 2 * XT_COLS), f)
    xT[:, 0:NODES] = x.T
    xT = np.ascontiguousarray(xT.reshape(D, -1, 2, 8 * P).transpose(2, 0, 1, 3)).reshape(2 * D, XT_COLS)
    w_edge = np.zeros((KF, D), f)
    w_edge[0:D] = w1[:, 0:D].T
    w_edge[D:D + EF] = w1[:, 2 * D:].T
    w_edge[D + EF] = np.asarray(L0_gnn_b1)
    low = (TILES // TS * GT + min(GT, LAST_TILES)) * P
    share = np.array([low / EDGES] * D + [(EDGES - low) / EDGES] * D, f).reshape(P, 1)
    k = np.arange(P)
    arrays = {
        "xT": xT, "xn": x, "src_cols": np.ascontiguousarray(src_p.reshape(SUPERS, TS, P).transpose(0, 2, 1)),
        "dst_cols": np.ascontiguousarray(dst_p.reshape(ALL_TILES, P).T),
        "dst_rows": dst_p.reshape(ROUNDS, SR * SUP), "edgeT": edge, "w_edge": w_edge,
        "w_dst": np.concatenate([w1[:, D:2 * D].T] * 2),
        "params": np.ascontiguousarray(np.stack([np.concatenate([c, c]) for c in cols], 1)),
        "wcol": share, "ident_in": np.eye(P, dtype=f), "fold_in": (k[:, None] % D == k[None, :] % D).astype(f),
        "nodecol_in": (k[:, None] + P * np.arange(NB)[None, :]).astype(f),
        "iota_in": np.broadcast_to(np.arange(WIN), (P, WIN)).astype(f),
    }
    nc = _bacc.Bacc("TRN2", target_bir_lowering=False, num_devices=1)
    args = [nc.dram_tensor(n, a.shape, mybir.dt.from_np(a.dtype), kind="ExternalInput").ap()
            for n, a in arrays.items()]
    args.append(nc.dram_tensor("out", (NODES, D), f32, kind="ExternalOutput").ap())
    gnn_kernel(nc, *args)
    r = _run(nc, [arrays], core_ids=[0])
    return r.results[0]["out"]
```

```python
import concourse.bass as bass
from concourse import mybir
from contextlib import ExitStack

NODES, EDGES, D, EF = 12500, 400000, 64, 41
P = 128
TS = 8
SUP = TS * P
SR = 4
COLS = SUP // 2
RC = SR * COLS
TILES = EDGES // P
ROUNDS = -(-EDGES // (SR * SUP))
SUPERS = ROUNDS * SR
ALL_TILES = SUPERS * TS
PAD_EDGES = SUPERS * SUP
LAST = TILES // TS
LAST_TILES = TILES - LAST * TS
NB = -(-NODES // P)
PAD_NODES = NB * P
GT = 4
GROUPS = ALL_TILES // GT
WIN = 64
AGG_COLS = PAD_NODES + 2 * WIN
assert NB % 2 == 0
XT_COLS = NB // 2 * P
KF = 112
EPS = 1e-5

f32 = mybir.dt.float32
bf16 = mybir.dt.bfloat16
i32 = mybir.dt.int32
ALU = mybir.AluOpType
ACT = mybir.ActivationFunctionType
AX = mybir.AxisListType

Y_MAX = 40.0
EXP_MAX = 1e18
HB = 9
HG = 3
EB = 3
PARTS = 3


def real_tiles(s):
    return max(0, min(TS, TILES - s * TS))


def gnn_kernel(nc, xT, xn, src_cols, dst_cols, dst_rows, edgeT, w_edge, w_dst, params, wcol,
               ident_in, fold_in, nodecol_in, iota_in, out):
    ctx = ExitStack()
    with ctx:
        def sb(name, shape, dt=f32, c=ctx):
            return c.enter_context(nc.sbuf_tensor(name, shape, dt))

        def pb(name, shape, c, dt=f32):
            return c.enter_context(nc.psum_tensor(name, shape, dt))

        def sem(name, c=ctx):
            return c.enter_context(nc.semaphore(name))

        z_dram = nc.dram_tensor("z_dram", [ROUNDS, P, RC], f32).ap()
        gmin_dram = nc.dram_tensor("gmin_dram", [ROUNDS, GROUPS // ROUNDS], i32).ap()
        gmax_dram = nc.dram_tensor("gmax_dram", [ROUNDS, GROUPS // ROUNDS], i32).ap()
        blk_dram = nc.dram_tensor("blk_dram", [ROUNDS, SR, 2], i32).ap()
        span_dram = nc.dram_tensor("span_dram", [ROUNDS, 1], i32).ap()

        ident = sb("ident", [P, P])
        fold = sb("fold", [P, P])
        par = sb("par", [P, 6])
        wc = sb("wc", [P, 2])
        gmin_row = sb("gmin_row", [1, GROUPS], i32)
        gmax_row = sb("gmax_row", [1, GROUPS], i32)
        span_row = sb("span_row", [1, ROUNDS], i32)
        careful = sb("careful", [1, 2], i32)
        dst_rel = sb("dst_rel", [P, ALL_TILES])
        coef1 = sb("coef1", [P, 2])
        coef2 = sb("coef2", [P, 2])
        coef3 = sb("coef3", [P, 2])
        stats = sb("stats", [P, LAST + 1, 6])
        iota = sb("iota", [P, WIN])

        c1 = ExitStack()
        with c1:
            blk_row = sb("blk_row", [1, 2 * SUPERS], i32, c1)
            w_e = sb("w_e", [KF, D], f32, c1)
            nodecol = sb("nodecol", [P, NB], f32, c1)
            pd = sb("pd", [P, NB, PARTS, D], bf16, c1)
            xT_s = sb("xT_s", [P, XT_COLS], f32, c1)
            w_d = sb("w_d", [P, 2 * D], f32, c1)
            dst_r = sb("dst_r", [ROUNDS, SR * SUP], i32, c1)
            dst_c = sb("dst_c", [P, ALL_TILES], i32, c1)
            gmin_b = sb("gmin_b", [P, GROUPS], i32, c1)
            gm = sb("gm", [ROUNDS, 2, GROUPS // ROUNDS], i32, c1)
            bl = sb("bl", [ROUNDS, SR, 2], i32, c1)
            bs = sb("bs", [ROUNDS, SR, 2], i32, c1)
            dif = sb("dif", [ROUNDS, GROUPS // ROUNDS], i32, c1)
            span = sb("span", [ROUNDS, 1], i32, c1)
            rest1 = sb("rest1", [P, 2, COLS], f32, c1)
            rest2 = sb("rest2", [P, 2, COLS], f32, c1)
            s_x, s_dr, s_dc, s_c, s_tab, s_row, s_gb, pd_mm, rng, first_part, less_one, second_part, less_two, \
                third_part, rel_done = (
                    sem(n, c1) for n in (
                        "s_x", "s_dr", "s_dc", "s_c", "s_tab", "s_row", "s_gb", "pd_mm", "rng", "first_part",
                        "less_one", "second_part", "less_two", "third_part", "rel_done"))
            src_ix = sb("src_ix", [P, SR, TS], i32, c1)
            G = sb("G", [P, SR, TS, D], f32, c1)
            xe = sb("xe", [KF, SR, SUP], f32, c1)
            dst_b = sb("dst_b", [P, SR, SUP], i32, c1)
            one_t = sb("one_t", [P, 2, SUP], bf16, c1)
            pd_cur = sb("pd_cur", [P, 2, PARTS, D], bf16, c1)
            zt = sb("zt", [P, SR, COLS], f32, c1)
            zero = sb("zero", [P, COLS], bf16, c1)
            ps_x = [pb(f"ps_x{i}", [D, SUP], c1) for i in range(2)]
            ps_z = [pb(f"ps_z{i}", [P, COLS], c1) for i in range(SR)]
            gathered = [sem(f"gathered{i}", c1) for i in range(SR)]
            src_in = [sem(f"src_in{i}", c1) for i in range(SR)]
            edge_in = [sem(f"edge_in{i}", c1) for i in range(SR)]
            dst_in = [sem(f"dst_in{i}", c1) for i in range(SR)]
            z_out = [sem(f"z_out{i}", c1) for i in range(SR)]
            XT_PIECE = COLS // D * P
            x_part = [sem(f"x_part{i}", c1) for i in range(-(-XT_COLS // XT_PIECE))]
            zeroed, one_ready, one_used, g_turned, xe_ready, z_done, zt_ready, counted, passed = (
                sem(n, c1) for n in ("zeroed", "one_ready", "one_used", "g_turned", "xe_ready", "z_done",
                                     "zt_ready", "counted", "passed"))
            KB = COLS // D
            banks = [(b, min(KB, NB - b)) for b in range(0, NB, KB)]
            b1 = c1.enter_context(nc.Block())

            def rounds(eng, body):
                body(0, True, False)
                with eng.Fori(1, ROUNDS - 1) as r:
                    body(r, False, False)
                body(ROUNDS - 1, False, True)

            def super_blocks(eng, s):
                _, v = nc.values_load_multi_w_load_instructions(
                    blk_row[0:1, bass.ds(s * 2, 2)], engines=[eng.engine], min_val=0, max_val=NB - 1)
                return v

            @b1.gpsimd
            def _(pool):
                def body(r, first, last):
                    for q in range(SR):
                        if not first:
                            pool.wait_ge(g_turned, r * SR + q - SR + 1)
                        pool.wait_ge(src_in[q], (r + 1) * 16)
                        pool.sem_inc(passed, 1)
                        for t in range(real_tiles(r * SR + q) if last else TS):
                            nc.gpsimd.indirect_dma_start(
                                out=G[:, q, t, :], out_offset=None, in_=xn,
                                in_offset=bass.IndirectOffsetOnAxis(ap=src_ix[:, q, t:t + 1], axis=0),
                            ).then_inc(gathered[q], 16)
                rounds(pool, body)

            @b1.sync
            def _(sp):
                def load_src(r, q, first):
                    if not first:
                        sp.wait_ge(gathered[q], r * (16 * TS))
                    sp.dma_start(src_ix[:, q, :], src_cols[bass.ds(r * SR + q, 1), :, :].rearrange(
                        "o p t -> (o p) t")).then_inc(src_in[q], 16)

                for q in range(SR):
                    load_src(0, q, True)
                sp.dma_start(dst_r[:], dst_rows).then_inc(s_dr, 16)
                sp.dma_start(w_d[:], w_dst).then_inc(s_x, 16)
                for i in range(len(x_part)):
                    c = slice(i * XT_PIECE, min((i + 1) * XT_PIECE, XT_COLS))
                    sp.dma_start(xT_s[:, c], xT[:, c]).then_inc(x_part[i], 16)
                for t, s in ((ident, ident_in), (w_e, w_edge), (nodecol, nodecol_in), (fold, fold_in),
                             (par, params), (wc, wcol), (iota, iota_in)):
                    sp.dma_start(t[:], s).then_inc(s_c, 16)
                sp.dma_start(dst_c[:], dst_cols).then_inc(s_dc, 16)
                sp.wait_ge(rng, 6)
                sp.dma_start(blk_dram, bs[:]).then_inc(s_tab, 16)
                sp.dma_start(gmin_dram, gm[:, 0, :]).then_inc(s_tab, 16)
                sp.dma_start(gmax_dram, gm[:, 1, :]).then_inc(s_tab, 16)
                sp.dma_start(span_dram, span[:]).then_inc(s_tab, 16)
                sp.wait_ge(s_tab, 64)
                for t, s, e in ((blk_row, blk_dram, "r s t -> (r s t)"), (gmin_row, gmin_dram, "r g -> (r g)"),
                                (gmax_row, gmax_dram, "r g -> (r g)"), (span_row, span_dram, "r o -> (r o)")):
                    sp.dma_start(t[:], s.rearrange(e)[None, :]).then_inc(s_row, 16)
                sp.dma_start(gmin_b[:], gmin_dram.rearrange("r g -> (r g)").partition_broadcast(P)
                             ).then_inc(s_gb, 16)

                def body(r, first, last):
                    for q in range(SR):
                        s = r * SR + q
                        if not first:
                            load_src(r, q, False)
                            sp.wait_ge(z_done, s - SR + 1)
                        sp.dma_start(xe[D:KF, q, :], edgeT[bass.ds(s, 1), :, :].rearrange("o k e -> (o k) e")
                                     ).then_inc(edge_in[q], 16)
                        if not first:
                            sp.wait_ge(counted, s - SR + 1)
                            sp.sem_inc(passed, 1)
                        sp.dma_start(dst_b[:, q, :],
                                     dst_rows[bass.ds(r, 1), q * SUP:(q + 1) * SUP].rearrange(
                                         "o e -> (o e)").partition_broadcast(P)).then_inc(dst_in[q], 16)
                rounds(sp, body)

            @b1.vector
            def _(dve):
                nc.vector.memset(zero[:], 0.0).then_inc(zeroed, 1)
                dve.wait_ge(s_dr, 16)
                by_group = dst_r[:].rearrange("r (g e) -> r g e", e=GT * P)
                nc.vector.tensor_reduce(gm[:, 0, :], by_group, AX.X, ALU.min).then_inc(rng, 1)
                nc.vector.tensor_reduce(gm[:, 1, :], by_group, AX.X, ALU.max).then_inc(rng, 1)
                dve.wait_ge(rng, 2)
                pairs = gm[:].rearrange("r m (s g) -> r m s g", g=TS // GT)
                nc.vector.tensor_tensor(bl[:, :, 0], pairs[:, 0, :, 0], pairs[:, 0, :, 1], ALU.min)
                nc.vector.tensor_tensor(bl[:, :, 1], pairs[:, 1, :, 0], pairs[:, 1, :, 1],
                                        ALU.max).then_inc(rng, 1)
                nc.vector.tensor_tensor(dif[:], gm[:, 1, :], gm[:, 0, :], ALU.subtract).then_inc(rng, 1)
                dve.wait_ge(rng, 4)
                nc.vector.tensor_single_scalar(bs[:], bl[:], 7, ALU.arith_shift_right).then_inc(rng, 1)
                nc.vector.tensor_reduce(span[:], dif[:], AX.X, ALU.max).then_inc(rng, 1)
                for i in range(len(banks) + 1):
                    if i < len(banks):
                        b0, n = banks[i]
                        dve.wait_ge(first_part, i + 1)
                        if i >= 2:
                            dve.wait_ge(second_part, i - 1)
                            dve.wait_ge(less_two, i - 1)
                        nc.vector.tensor_tensor(
                            rest1[:, i % 2, 0:n * D].rearrange("p (b d) -> p b d", d=D),
                            ps_z[i % SR][:, 0:n * D].rearrange("p (b d) -> p b d", d=D),
                            pd[:, b0:b0 + n, 0, :], ALU.subtract).then_inc(less_one, 1)
                    if i >= 1:
                        j = i - 1
                        b0, n = banks[j]
                        dve.wait_ge(second_part, j + 1)
                        if j >= 2:
                            dve.wait_ge(third_part, j - 1)
                        nc.vector.tensor_tensor(
                            rest2[:, j % 2, 0:n * D].rearrange("p (b d) -> p b d", d=D),
                            rest1[:, j % 2, 0:n * D].rearrange("p (b d) -> p b d", d=D),
                            pd[:, b0:b0 + n, 1, :], ALU.subtract).then_inc(less_two, 1)
                dve.wait_ge(third_part, len(banks))
                dve.wait_ge(s_row, 64)
                dve.wait_ge(s_c, 112)

                made = dve.alloc_register("marks_made")
                before = dve.alloc_register("marks_before")
                dve.reg_mov(made, 1)
                dve.reg_mov(before, 1)

                def marks(r, q):
                    s = r * SR + q
                    lo, hi = super_blocks(dve, s)
                    dve.wait_ge(dst_in[q], (r + 1) * 16)
                    dve.sem_inc(passed, 1)
                    dve.wait_ge(one_used, dve.snap(before, min_val=1))
                    dve.sem_inc(passed, 1)
                    dve.reg_mov(before, made)
                    with dve.Fori(lo, hi + 1) as b:
                        nc.vector.tensor_copy(pd_cur[:, q % 2, :, :],
                                              pd[:, bass.ds(b, 1), :, :].rearrange("p o k d -> p (o k) d"))
                        nc.vector.tensor_scalar(one_t[:, q % 2, :], dst_b[:, q, :],
                                                nodecol[:, bass.ds(b, 1)], None,
                                                ALU.is_equal).then_inc(one_ready, 1)
                        dve.reg_add(made, made, 1)
                        dve.wait_ge(one_used, dve.snap(made, min_val=1))

                def body(r, first, last):
                    for q in range(SR):
                        s = r * SR + q
                        if q + 1 < SR:
                            marks(r, q + 1)
                        elif not last:
                            marks(r + 1, 0)
                        dve.wait_ge(zt_ready, s + 1)
                        if not last or s < LAST:
                            nc.vector.bn_stats(stats[:, bass.ds(s, 1), :], zt[:, q, :]).then_inc(counted, 1)
                        elif s == LAST:
                            low, high = min(GT, LAST_TILES) * P, max(0, LAST_TILES - GT) * P
                            nc.vector.bn_stats(stats[0:D, s, :], zt[0:D, q, 0:low])
                            nc.vector.bn_stats(stats[D:P, s, :], zt[D:P, q, 0:high]).then_inc(counted, 1)
                marks(0, 0)
                dve.wait_ge(s_gb, 16)
                dve.wait_ge(s_dc, 16)
                nc.vector.tensor_tensor(dst_rel[:].rearrange("p (g t) -> p g t", t=GT),
                                        dst_c[:].rearrange("p (g t) -> p g t", t=GT),
                                        gmin_b[:].rearrange("p (g o) -> p g o", o=1).to_broadcast(
                                            [P, GROUPS, GT]), ALU.subtract).then_inc(rel_done, 1)
                rounds(dve, body)

            @b1.tensor
            def _(pe):
                pe.wait_ge(s_x, 16)
                for i, (b0, n) in enumerate(banks):
                    if i % 2 == 0:
                        pe.wait_ge(x_part[i // 2], 16)
                    if i >= SR:
                        pe.wait_ge(less_one, i - SR + 1)
                    for k in range(0, n, 2):
                        c = (b0 + k) // 2 * P
                        m = nc.tensor.matmul(ps_z[i % SR][:, k * D:(k + 2) * D], xT_s[:, c:c + P], w_d[:],
                                             start=True, stop=True)
                    m.then_inc(pd_mm, 1)
                pe.wait_ge(less_one, len(banks))
                pe.wait_ge(zeroed, 1)
                pe.wait_ge(s_row, 64)
                pe.wait_ge(s_c, 112)
                pe.sem_inc(one_used, 1)
                seen = pe.alloc_register("marks_seen")
                pe.reg_mov(seen, 0)

                def from_dst(r, q, early):
                    s = r * SR + q
                    z = ps_z[q]
                    lo, hi = super_blocks(pe, s)
                    if not early:
                        pe.wait_ge(zt_ready, s - SR + 1)
                    for o in range(2):
                        nc.tensor.matmul(z[o * D:(o + 1) * D, :], zero[:, 0:D], zero[:], start=True, stop=False)
                    with pe.Fori(lo, hi + 1):
                        pe.reg_add(seen, seen, 1)
                        pe.wait_ge(one_ready, pe.snap(seen, min_val=1))
                        for part in range(PARTS):
                            for o in range(2):
                                m = nc.tensor.matmul(z[o * D:(o + 1) * D, :], pd_cur[:, q % 2, part, :],
                                                     one_t[:, q % 2, o * COLS:(o + 1) * COLS],
                                                     start=False, stop=False)
                        m.then_inc(one_used, 1)

                def body(r, first, last):
                    for q in range(SR):
                        s = r * SR + q
                        if not first or q >= 2:
                            pe.wait_ge(xe_ready, s - 1)
                        new = real_tiles(s) if last else TS
                        pe.wait_ge(gathered[q], r * (16 * TS) + 16 * new)
                        pe.sem_inc(passed, 1)
                        for t in range(TS):
                            m = nc.tensor.transpose(ps_x[q % 2][:, t * P:(t + 1) * P], G[:, q, t, :], ident[:])
                        m.then_inc(g_turned, 1)
                        if q + 1 < SR:
                            from_dst(r, q + 1, first)
                        elif not last:
                            from_dst(r + 1, 0, False)
                        pe.wait_ge(xe_ready, s + 1)
                        pe.wait_ge(edge_in[q], (r + 1) * 16)
                        for o in range(2):
                            m = nc.tensor.matmul(ps_z[q][o * D:(o + 1) * D, :], w_e[:],
                                                 xe[:, q, o * COLS:(o + 1) * COLS], start=False, stop=True)
                        m.then_inc(z_done, 1)
                from_dst(0, 0, True)
                rounds(pe, body)

            @b1.scalar
            def _(act):
                for i in range(len(banks) + 2):
                    if i < len(banks):
                        b0, n = banks[i]
                        act.wait_ge(pd_mm, i + 1)
                        nc.scalar.copy(pd[:, b0:b0 + n, 0, :],
                                       ps_z[i % SR][:, 0:n * D].rearrange("p (b d) -> p b d", d=D)
                                       ).then_inc(first_part, 1)
                    if 1 <= i <= len(banks):
                        j = i - 1
                        b0, n = banks[j]
                        act.wait_ge(less_one, j + 1)
                        nc.scalar.copy(pd[:, b0:b0 + n, 1, :],
                                       rest1[:, j % 2, 0:n * D].rearrange("p (b d) -> p b d", d=D)
                                       ).then_inc(second_part, 1)
                    if i >= 2:
                        j = i - 2
                        b0, n = banks[j]
                        act.wait_ge(less_two, j + 1)
                        nc.scalar.copy(pd[:, b0:b0 + n, 2, :],
                                       rest2[:, j % 2, 0:n * D].rearrange("p (b d) -> p b d", d=D)
                                       ).then_inc(third_part, 1)

                def body(r, first, last):
                    for q in range(SR):
                        s = r * SR + q
                        act.wait_ge(g_turned, s + 1)
                        if not first:
                            act.wait_ge(z_done, s - SR + 1)
                        nc.scalar.copy(xe[0:D, q, :], ps_x[q % 2][:]).then_inc(xe_ready, 1)
                        act.wait_ge(z_done, s + 1)
                        if not first:
                            act.wait_ge(z_out[q], r * 16)
                            act.wait_ge(counted, s - SR + 1)
                        nc.scalar.copy(zt[:, q, :], ps_z[q][:]).then_inc(zt_ready, 1)
                        act.wait_ge(zt_ready, s + 1)
                        act.dma_start(z_dram[bass.ds(r, 1), :, q * COLS:(q + 1) * COLS].rearrange(
                            "o p c -> (o p) c"), zt[:, q, :]).then_inc(z_out[q], 16)
                rounds(act, body)
                for q in range(SR):
                    act.wait_ge(z_out[q], ROUNDS * 16)

        def coefficients(name, coef, gamma, beta, stats, share, bound=None, meanwhile=None):
            c = ExitStack()
            with c:
                v = sb(name + "_v", [P, 14], f32, c)
                top = sb(name + "_top", [1, 1], f32, c)
                ps = pb(name + "_ps", [P, 2], c)
                ps_b = pb(name + "_ps_b", [1, P], c)
                done, summed, rooted = sem(name + "_done", c), sem(name + "_summed", c), sem(name + "_rooted", c)
                blk = c.enter_context(nc.Block())

                @blk.vector
                def _(dve):
                    n = [0]

                    def then(i):
                        n[0] += 1
                        i.then_inc(done, 1)
                        dve.wait_ge(done, n[0])

                    nc.vector.memset(v[:, 2:14], 0.0)
                    then(nc.vector.bn_aggr(v[:, 0:2], stats[:].rearrange("p s k -> p (s k)")))
                    then(nc.vector.tensor_tensor(v[:, 2:3], v[:, 0:1], share, ALU.mult))
                    dve.wait_ge(summed, 1)
                    then(nc.vector.tensor_copy(v[:, 3:4], ps[:, 0:1]))
                    then(nc.vector.tensor_tensor(v[:, 4:5], v[:, 0:1], v[:, 3:4], ALU.subtract))
                    then(nc.vector.tensor_tensor(v[:, 5:6], v[:, 4:5], v[:, 4:5], ALU.mult))
                    then(nc.vector.tensor_tensor(v[:, 6:7], v[:, 5:6], v[:, 1:2], ALU.add))
                    then(nc.vector.tensor_tensor(v[:, 7:8], v[:, 6:7], share, ALU.mult))
                    dve.wait_ge(summed, 2)
                    then(nc.vector.tensor_scalar(v[:, 8:9], ps[:, 1:2], EPS, None, ALU.add))
                    dve.wait_ge(rooted, 1)
                    then(nc.vector.reciprocal(v[:, 10:11], v[:, 9:10]))
                    then(nc.vector.tensor_tensor(coef[:, 0:1], v[:, 10:11], par[:, gamma:gamma + 1], ALU.mult))
                    then(nc.vector.tensor_tensor(v[:, 11:12], v[:, 3:4], coef[:, 0:1], ALU.mult))
                    then(nc.vector.tensor_tensor(coef[:, 1:2], par[:, beta:beta + 1], v[:, 11:12], ALU.subtract))
                    if bound is not None:
                        then(nc.vector.tensor_tensor(v[:, 12:13], coef[:, 0:1], coef[:, 1:2], ALU.add))
                        then(nc.vector.tensor_tensor(v[:, 13:14], v[:, 12:13], coef[:, 1:2], ALU.max))
                        dve.wait_ge(summed, 3)
                        then(nc.vector.tensor_reduce(top[:], ps_b[:], AX.X, ALU.max))
                        then(nc.vector.tensor_scalar(bound, top[:], Y_MAX, None, ALU.is_gt))

                @blk.tensor
                def _(pe):
                    pe.wait_ge(done, 2)
                    nc.tensor.matmul(ps[:, 0:1], fold[:], v[:, 2:3], start=True, stop=True).then_inc(summed, 1)
                    pe.wait_ge(done, 7)
                    nc.tensor.matmul(ps[:, 1:2], fold[:], v[:, 7:8], start=True, stop=True).then_inc(summed, 1)
                    if bound is not None:
                        pe.wait_ge(done, 14)
                        nc.tensor.matmul(ps_b[:], v[:, 13:14], ident[:], start=True, stop=True).then_inc(summed, 1)

                @blk.sync
                def _(sp):
                    if meanwhile is not None:
                        meanwhile(sp)

                @blk.scalar
                def _(act):
                    act.wait_ge(done, 8)
                    nc.scalar.activation(v[:, 9:10], v[:, 8:9], ACT.Sqrt).then_inc(rooted, 1)

        LAST_BODY = (ROUNDS - 1) // HB * HB
        HELD = ROUNDS - LAST_BODY
        agg = sb("agg", [P, AGG_COLS])
        cf = ExitStack()
        f = sb("f", [P, HB, RC], f32, cf)
        z_in = [sem(f"z_in{i}", cf) for i in range(HB)]

        def first_loads(sp):
            for k in range(HB):
                sp.dma_start(f[:, k, :], z_dram[k]).then_inc(z_in[k], 16)

        coefficients("bn1", coef1, 0, 1, stats, wc[:, 0:1], meanwhile=first_loads)

        c2 = ExitStack()
        with c2:
            top = sb("span_top", [1, 1], i32, c2)
            widest = sem("widest", c2)
            f_ready, f_counted = sem("f_ready", c2), sem("f_counted", c2)
            b2 = c2.enter_context(nc.Block())

            def in_bodies(eng, body):
                body(0, HB, True, False)
                with eng.Fori(HB, LAST_BODY - HB + 1, HB) as r0:
                    body(r0, HB, False, False)
                body(LAST_BODY, HELD, False, True)

            @b2.sync
            def _(sp):
                def body(r0, n, first, last):
                    if first:
                        return
                    for k in range(n):
                        sp.wait_ge(f_counted, r0 + k - HB + 1)
                        sp.dma_start(f[:, k, :], z_dram[bass.ds(r0 + k, 1), :, :].rearrange(
                            "o p c -> (o p) c")).then_inc(z_in[k], 16)
                in_bodies(sp, body)

            @b2.gpsimd
            def _(pool):
                nc.gpsimd.memset(agg[:], 0.0)

            @b2.scalar
            def _(act):
                def body(r0, n, first, last):
                    for k in range(n):
                        act.wait_ge(z_in[k], (r0 // HB) * 16 + 16)
                        nc.scalar.activation(f[:, k, :], f[:, k, :], ACT.Sigmoid, bias=coef1[:, 1:2],
                                             scale=coef1[:, 0:1]).then_inc(f_ready, 1)
                in_bodies(act, body)

            @b2.vector
            def _(dve):
                nc.vector.tensor_reduce(top[:], span_row[:], AX.X, ALU.max).then_inc(widest, 1)
                dve.wait_ge(widest, 1)
                nc.vector.tensor_scalar(careful[:, 1:2], top[:], WIN - 1, None, ALU.is_gt)

                def body(r0, n, first, last):
                    for k in range(n):
                        dve.wait_ge(f_ready, r0 + k + 1)
                        for q in range(SR):
                            s = (r0 + k) * SR + q
                            v = f[:, k, q * COLS:(q + 1) * COLS]
                            if not last or s < LAST:
                                m = nc.vector.bn_stats(stats[:, bass.ds(s, 1), :], v)
                            elif s == LAST:
                                low, high = min(GT, LAST_TILES) * P, max(0, LAST_TILES - GT) * P
                                nc.vector.bn_stats(stats[0:D, s, :], v[0:D, 0:low])
                                m = nc.vector.bn_stats(stats[D:P, s, :], v[D:P, 0:high])
                        m.then_inc(f_counted, 1)
                in_bodies(dve, body)

        coefficients("bn2", coef2, 2, 3, stats, wc[:, 0:1], careful[:, 0:1])

        c3 = ExitStack()
        YC = RC // 4
        with c3:
            e = sb("e", [P, EB, RC], f32, c3)
            y = sb("y", [P, YC], f32, c3)
            ht = sb("ht", [P, 2, 2 * GT, 2, D], f32, c3)
            oh = sb("oh", [P, 2, 2 * TS, WIN], f32, c3)
            xrel = sb("xrel", [P, GT], f32, c3)
            ohx = sb("ohx", [P, GT, WIN], f32, c3)
            ps_h = [pb(f"ps_h{i}", [P, 2 * COLS], c3) for i in range(2)]
            ps_a = [pb(f"ps_a{i}", [P, COLS], c3) for i in range(2)]
            ps_e = pb("ps_e", [P, COLS], c3)
            z_in = [sem(f"z_in3{i}", c3) for i in range(HB)]
            (sig_done, exp_done, clamped, ln_done, sp_done, h_done, h_turned, ht_ready, oh_ready,
             summed, added, more_oh, more_sum, passed3) = (sem(n, c3) for n in (
                 "sig_done", "exp_done", "clamped", "ln_done", "sp_done", "h_done", "h_turned",
                 "ht_ready", "oh_ready", "summed", "added", "more_oh", "more_sum", "passed3"))
            assert HB % EB == 0 and TILES > (ROUNDS * SR // 2 - 1) * 2 * TS
            UG = 2 * TS // GT
            b3 = c3.enter_context(nc.Block())

            def in_bodies(eng, body):
                body(LAST_BODY, 0, HELD, "held")
                body(0, HELD, HB, "second")
                with eng.Fori(HB, LAST_BODY - 2 * HB + 1, HB) as r0:
                    body(r0, r0 + HELD, HB, "middle")
                body(LAST_BODY - HB, ROUNDS - HB, HB, "last")

            def unit_of(r0, p0, k, half, where):
                return r0 + k, p0 + k, half, k if where == "held" else HELD + k

            def before(r0, p0, k, half, where):
                if half:
                    return unit_of(r0, p0, k, 0, where)
                if k:
                    return unit_of(r0, p0, k - 1, 1, where)
                if where == "held":
                    return None
                if where == "second":
                    return LAST_BODY + HELD - 1, HELD - 1, 1, HELD - 1
                return r0 - 1, p0 - 1, 1, HELD

            def after(r0, p0, n, k, half, where):
                if half == 0:
                    return unit_of(r0, p0, k, 1, where)
                if k + 1 < n:
                    return unit_of(r0, p0, k + 1, 0, where)
                if where == "held":
                    return 0, HELD, 0, HELD
                return None if where == "last" else (r0 + n, p0 + n, 0, HELD)

            LAST_UNIT = (LAST_BODY - 1, ROUNDS - 1, 1, ROUNDS - 1)

            def exp_slot(p0, k, where):
                return k % EB if where == "held" else (HELD + k) % EB

            def tiles_in(u, g):
                return max(0, min(GT, TILES - (u * UG + g) * GT)) if isinstance(u, int) else GT

            def group_range(eng, g):
                return (eng.value_load(gmin_row[0:1, bass.ds(g, 1)], min_val=0, max_val=NODES - 1),
                        eng.value_load(gmax_row[0:1, bass.ds(g, 1)], min_val=0, max_val=NODES - 1))

            def is_wide(eng, r):
                return eng.value_load(span_row[0:1, bass.ds(r, 1)], min_val=0, max_val=NODES)

            def in_variants(eng, program):
                _, (high, wide) = nc.values_load_multi_w_load_instructions(
                    careful[:], engines=[eng.engine], min_val=0, max_val=1)
                either = eng.snap(high + wide, min_val=0, max_val=2)
                with eng.If(either > 0):
                    program(high, wide)
                with eng.Else():
                    program(None, None)

            @b3.sync
            def _(sp):
                def body(r0, p0, n, where):
                    if where == "held":
                        return
                    for k in range(n):
                        if where != "second":
                            sp.wait_ge(h_turned, (p0 + k - HB) * 2 + 2)
                        elif k < HELD:
                            sp.wait_ge(h_turned, k * 2 + 2)
                        sp.dma_start(f[:, k, :], z_dram[bass.ds(r0 + k, 1), :, :].rearrange(
                            "o p c -> (o p) c")).then_inc(z_in[k], 16)
                in_bodies(sp, body)

            @b3.scalar
            def _(act):
                def program(high, wide):
                    def sigmoids(r0, k0, k1):
                        for k in range(k0, k1):
                            act.wait_ge(z_in[k], (r0 // HB) * 16 + 16)
                            nc.scalar.activation(f[:, k, :], f[:, k, :], ACT.Sigmoid, bias=coef1[:, 1:2],
                                                 scale=coef1[:, 0:1]).then_inc(sig_done, 1)

                    def logs(r0, p0, k0, k1, where):
                        nc.scalar.preload_act_table_set("natural_log_exp_and_others")
                        for k in range(k0, k1):
                            p = p0 + k
                            s = exp_slot(p0, k, where)
                            if where != "held":
                                act.wait_ge(sig_done, r0 + k + 1)
                            if where != "held" or k >= EB:
                                act.wait_ge(h_done, p - EB + 1)
                            nc.scalar.activation(e[:, s, :], f[:, k, :], ACT.Exp, bias=coef2[:, 1:2],
                                                 scale=coef2[:, 0:1]).then_inc(exp_done, 1)
                            if high is not None:
                                with act.If(high > 0):
                                    act.wait_ge(clamped, p + 1)
                                    act.sem_inc(passed3, 1)
                            act.wait_ge(exp_done, p + 1)
                            nc.scalar.activation(e[:, s, :], e[:, s, :], ACT.Ln, bias=1.0).then_inc(ln_done, 1)

                    def body(r0, p0, n, where):
                        if where == "held":
                            logs(r0, p0, 0, n - HG, where)
                            sigmoids(0, 0, HG)
                            logs(r0, p0, n - HG, n, where)
                            return
                        for k0 in range(0, n, HG):
                            if k0 + HG < n:
                                sigmoids(r0, k0 + HG, k0 + 2 * HG)
                            elif where != "last":
                                sigmoids(r0 + HB, 0, HG)
                            logs(r0, p0, k0, k0 + HG, where)
                    in_bodies(act, body)
                in_variants(act, program)

            @b3.gpsimd
            def _(pool):
                def program(high, wide):
                    def body(r0, p0, n, where):
                        for k in range(n):
                            p = p0 + k
                            if high is not None:
                                with pool.If(high > 0):
                                    pool.wait_ge(sp_done, p + 1)
                                    pool.sem_inc(passed3, 1)
                            pool.wait_ge(ln_done, p + 1)
                            nc.gpsimd.tensor_tensor(f[:, k, :], e[:, exp_slot(p0, k, where), :], f[:, k, :],
                                                    ALU.mult).then_inc(h_done, 1)
                    in_bodies(pool, body)
                in_variants(pool, program)

            @b3.vector
            def _(dve):
                dve.sem_inc(added, 2)
                extra = dve.alloc_register("extra_windows")
                dve.reg_mov(extra, 0)

                def program(high, wide):
                    def mark(r, p, half, low):
                        u = r * 2 + half
                        if low >= 1:
                            dve.wait_ge(summed, p * 2 + half - 1)
                        rel = dst_rel[:, bass.ds(u * (2 * TS), 2 * TS)]
                        nc.vector.tensor_tensor(
                            oh[:, half, :, :],
                            rel.rearrange("p (t o) -> p t o", o=1).to_broadcast([P, 2 * TS, WIN]),
                            iota[:].rearrange("p (o w) -> p o w", o=1).to_broadcast([P, 2 * TS, WIN]),
                            ALU.is_equal).then_inc(oh_ready, 1)

                    def starts(r, p, half, low):
                        return nc.values_load_multi_w_load_instructions(
                            gmin_row[0:1, bass.ds((r * 2 + half) * UG, UG)], engines=[dve.engine],
                            min_val=0, max_val=NODES - 1,
                            skip_runtime_bounds_check_because="dst is the number of a node")[1]

                    def add(r, p, half, low, at):
                        u, i = r * 2 + half, p * 2 + half
                        dve.wait_ge(summed, i + 1)
                        for g in range(UG):
                            rows = slice(g % 2 * D, g % 2 * D + D)
                            v = agg[rows, bass.ds(at[g], WIN)]
                            if tiles_in(u, g):
                                dve.wait_ge(added, i * UG + g + 1)
                                nc.vector.tensor_tensor(v, v, ps_a[half][rows, g // 2 * WIN:(g // 2 + 1) * WIN],
                                                        ALU.add).then_inc(added, 1)
                            else:
                                dve.wait_ge(added, i * UG + g + 2)
                                dve.sem_inc(added, 1)
                        more_windows(r, u)

                    def more_windows(r, u):
                        if wide is not None:
                            with dve.If(wide > 0), dve.If(is_wide(dve, r) > WIN - 1):
                                for g in range(UG):
                                    if not tiles_in(u, g):
                                        continue
                                    rows = slice(g % 2 * D, g % 2 * D + D)
                                    lo, hi = group_range(dve, u * UG + g)
                                    dve.drain()
                                    nc.vector.tensor_copy(xrel[:], dst_rel[:, bass.ds((u * UG + g) * GT, GT)])
                                    with dve.Fori(lo + WIN, hi + 1, WIN) as w:
                                        dve.drain()
                                        nc.vector.tensor_scalar(xrel[:], xrel[:], -float(WIN), None, ALU.add)
                                        dve.drain()
                                        nc.vector.tensor_tensor(
                                            ohx[:], xrel[:].rearrange("p (t o) -> p t o", o=1).to_broadcast([P, GT, WIN]),
                                            iota[:].rearrange("p (o w) -> p o w", o=1).to_broadcast([P, GT, WIN]),
                                            ALU.is_equal).then_inc(more_oh, 1)
                                        dve.reg_add(extra, extra, 1)
                                        dve.wait_ge(more_sum, dve.snap(extra, min_val=1))
                                        v = agg[rows, bass.ds(w, WIN)]
                                        nc.vector.tensor_tensor(v, v, ps_e[rows, 0:WIN], ALU.add)
                                dve.drain()

                    def turn_out(r, p, half, low):
                        i = p * 2 + half
                        dve.wait_ge(h_turned, i + 1)
                        if low >= 1:
                            dve.wait_ge(summed, i - 1)
                        nc.vector.tensor_copy(ht[:, half, :, :, :].rearrange("p t o d -> p (t o d)"),
                                              ps_h[half][:]).then_inc(ht_ready, 1)

                    def softplus(p, k, s):
                        if high is not None:
                            with dve.If(high > 0):
                                dve.wait_ge(exp_done, p + 1)
                                nc.vector.tensor_scalar(e[:, s, :], e[:, s, :], EXP_MAX, None, ALU.min).then_inc(clamped, 1)
                                dve.wait_ge(ln_done, p + 1)
                                dve.sem_inc(passed3, 1)
                                for c in range(0, RC, YC):
                                    dve.drain()
                                    nc.vector.tensor_scalar(y[:], f[:, k, c:c + YC], coef2[:, 0:1], coef2[:, 1:2],
                                                            ALU.mult, ALU.add)
                                    dve.drain()
                                    v = e[:, s, c:c + YC]
                                    m = nc.vector.tensor_tensor(v, v, y[:], ALU.max)
                                m.then_inc(sp_done, 1)

                    def body(r0, p0, n, where):
                        for k in range(n):
                            for half in range(2):
                                prev, following = before(r0, p0, k, half, where), after(r0, p0, n, k, half, where)
                                turn_out(*unit_of(r0, p0, k, half, where))
                                at = starts(*prev) if prev else None
                                if following:
                                    mark(*following)
                                if prev:
                                    add(*prev, at)
                            if k + 1 < n:
                                softplus(p0 + k + 1, k + 1, exp_slot(p0, k + 1, where))
                            elif where != "last":
                                softplus(p0 + n, 0, HELD % EB)
                    softplus(0, 0, 0)
                    mark(LAST_BODY, 0, 0, 0)
                    in_bodies(dve, body)
                    add(*LAST_UNIT, starts(*LAST_UNIT))
                in_variants(dve, program)

            @b3.tensor
            def _(pe):
                extra = pe.alloc_register("extra_windows_pe")
                pe.reg_mov(extra, 0)

                def program(high, wide):
                    def turn(r, p, half, low, slot):
                        if half == 0:
                            pe.wait_ge(h_done, p + 1)
                        if low >= 1:
                            pe.wait_ge(ht_ready, p * 2 + half - 1)
                        for j in range(2 * GT):
                            col = half * 2 * COLS + j * P
                            m = nc.tensor.transpose(ps_h[half][:, j * P:(j + 1) * P],
                                                    f[:, slot, col:col + P], ident[:])
                        m.then_inc(h_turned, 1)

                    def sum_up(r, p, half, low):
                        u, i = r * 2 + half, p * 2 + half
                        pe.wait_ge(ht_ready, i + 1)
                        pe.wait_ge(oh_ready, i + 1)
                        if low >= 1:
                            pe.wait_ge(added, (i - 1) * UG + 2)
                        for g in range(UG):
                            n = tiles_in(u, g)
                            rows = slice(g % 2 * D, g % 2 * D + D)
                            for t in range(n):
                                m = nc.tensor.matmul(ps_a[half][rows, g // 2 * WIN:(g // 2 + 1) * WIN],
                                                     ht[:, half, g // 2 * GT + t, g % 2, :],
                                                     oh[:, half, g * GT + t, :], start=(t == 0), stop=(t == n - 1))
                        m.then_inc(summed, 1)
                        if wide is not None:
                            with pe.If(wide > 0), pe.If(is_wide(pe, r) > WIN - 1):
                                for g in range(UG):
                                    n = tiles_in(u, g)
                                    if not n:
                                        continue
                                    rows = slice(g % 2 * D, g % 2 * D + D)
                                    lo, hi = group_range(pe, u * UG + g)
                                    with pe.Fori(lo + WIN, hi + 1, WIN):
                                        pe.reg_add(extra, extra, 1)
                                        pe.wait_ge(more_oh, pe.snap(extra, min_val=1))
                                        for t in range(n):
                                            m = nc.tensor.matmul(ps_e[rows, 0:WIN],
                                                                 ht[:, half, g // 2 * GT + t, g % 2, :],
                                                                 ohx[:, t, :], start=(t == 0), stop=(t == n - 1))
                                        m.then_inc(more_sum, 1)
                                pe.nop()

                    def body(r0, p0, n, where):
                        for k in range(n):
                            for half in range(2):
                                turn(*unit_of(r0, p0, k, half, where), k)
                                prev = before(r0, p0, k, half, where)
                                if prev:
                                    sum_up(*prev)
                    in_bodies(pe, body)
                    sum_up(*LAST_UNIT)
                in_variants(pe, program)
        cf.close()

        HALF = NODES // 2
        HBLOCKS = -(-HALF // P)
        FULL = HALF // P
        REST = HALF - FULL * P
        NS = -(-HALF // COLS)
        total = sb("total", [P, HBLOCKS * P])
        x_s = sb("x_s", [P, 2 * HBLOCKS, D])
        st = sb("st", [P, NS, 6])
        x_in, cleared = sem("x_in"), sem("cleared")

        def of_half(a, b0, b1, h):
            return a[:, b0:b1, :].rearrange("p (j h) d -> p j h d", h=2)[:, :, h, :]

        c5 = ExitStack()
        with c5:
            ps_s = [pb(f"ps_s{i}", [P, COLS], c5) for i in range(4)]
            folded, moved = sem("folded", c5), sem("moved", c5)
            b5 = c5.enter_context(nc.Block())

            def width(j):
                return min(COLS, HALF - j * COLS)

            @b5.gpsimd
            def _(pool):
                nc.gpsimd.memset(x_s[96:P, 2 * FULL:, :], 0.0).then_inc(cleared, 1)
                pool.wait_ge(cleared, 1)
                nc.gpsimd.memset(total[:, HALF:], 0.0).then_inc(cleared, 1)

            @b5.sync
            def _(sp):
                for h in range(2):
                    n0 = HALF * h
                    sp.dma_start(of_half(x_s, 0, 2 * FULL, h), xn[n0:n0 + FULL * P, :].rearrange(
                        "(b p) d -> p b d", p=P)).then_inc(x_in, 16)
                sp.wait_ge(cleared, 1)
                for h in range(2):
                    n0 = HALF * h + FULL * P
                    sp.dma_start(x_s[0:REST, 2 * FULL + h, :], xn[n0:n0 + REST, :]).then_inc(x_in, 16)

            @b5.tensor
            def _(pe):
                for j in range(NS):
                    if j >= 4:
                        pe.wait_ge(moved, j - 3)
                    for h in range(2):
                        c = HALF * h + j * COLS
                        m = nc.tensor.matmul(ps_s[j % 4][h * D:h * D + D, 0:width(j)], fold[:, 0:D],
                                             agg[:, c:c + width(j)], start=True, stop=True)
                    m.then_inc(folded, 1)

            @b5.vector
            def _(dve):
                for j in range(NS):
                    dve.wait_ge(moved, j + 1)
                    nc.vector.bn_stats(st[:, j, :], total[:, j * COLS:j * COLS + width(j)])

            @b5.scalar
            def _(act):
                for j in range(NS):
                    act.wait_ge(folded, j + 1)
                    nc.scalar.copy(total[:, j * COLS:j * COLS + width(j)],
                                   ps_s[j % 4][:, 0:width(j)]).then_inc(moved, 1)

        coefficients("bn3", coef3, 4, 5, st, wc[:, 1:2])

        c4 = ExitStack()
        with c4:
            v = sb("v", [P, 2 * HBLOCKS, D], f32, c4)
            w = sb("w", [P, 2 * HBLOCKS, D], f32, c4)
            ln = sb("ln", [P, 5, 2 * HBLOCKS], f32, c4)
            KB = COLS // D
            banks = [(b, min(KB, 2 * HBLOCKS - b)) for b in range(0, 2 * HBLOCKS, KB)]
            pieces = [(0, 4), (4, 8), (8, 11), (11, len(banks))]
            spans = [(banks[a][0], banks[b - 1][0] + banks[b - 1][1]) for a, b in pieces]
            ps_n = [pb(f"ps_n{i}", [P, COLS], c4) for i in range(4)]
            (o_out, normalised, d, turned, copied, centred, squared, spread, rooted, inverted, normed) = (
                sem(n, c4) for n in ("o_out", "normalised", "d4", "turned4", "copied4", "centred", "squared",
                                     "spread", "rooted", "inverted", "normed"))
            b4 = c4.enter_context(nc.Block())

            def wide(a, b0, b1):
                return a[:, b0:b1].rearrange("p (b o) -> p b o", o=1).to_broadcast([P, b1 - b0, D])

            @b4.sync
            def _(sp):
                for i, (b0, b1) in enumerate(spans):
                    sp.wait_ge(normed, i + 1)
                    e = min(b1, 2 * FULL)
                    for h in range(2):
                        n0 = HALF * h
                        sp.dma_start(out[n0 + b0 // 2 * P:n0 + e // 2 * P, :].rearrange("(b p) d -> p b d", p=P),
                                     of_half(v, b0, e, h)).then_inc(o_out, 16)
                for h in range(2):
                    n0 = HALF * h + FULL * P
                    sp.dma_start(out[n0:n0 + REST, :], v[0:REST, 2 * FULL + h, :]).then_inc(o_out, 16)
                sp.wait_ge(o_out, 32 * len(spans) + 32)

            @b4.gpsimd
            def _(pool):
                for i, (b0, b1) in enumerate(spans):
                    pool.wait_ge(inverted, i + 1)
                    nc.gpsimd.tensor_tensor(v[:, b0:b1, :], v[:, b0:b1, :], wide(ln[:, 4, :], b0, b1),
                                            ALU.mult).then_inc(normed, 1)

            @b4.scalar
            def _(act):
                def normalise(i):
                    b0, n = banks[i]
                    t = total[:, b0 // 2 * P:(b0 + n) // 2 * P]
                    nc.scalar.activation(t, t, ACT.Identity, bias=coef3[:, 1:2],
                                         scale=coef3[:, 0:1]).then_inc(normalised, 1)

                for i in range(*pieces[0]):
                    normalise(i)
                for p, (b0, b1) in enumerate(spans):
                    if p + 1 < len(spans):
                        for i in range(*pieces[p + 1]):
                            normalise(i)
                    act.wait_ge(centred, p + 1)
                    nc.scalar.activation(w[:, b0:b1, :], v[:, b0:b1, :], ACT.Square).then_inc(squared, 1)
                    act.wait_ge(spread, 2 * p + 2)
                    nc.scalar.activation(ln[:, 3, b0:b1], ln[:, 2, b0:b1], ACT.Sqrt).then_inc(rooted, 1)

            @b4.tensor
            def _(pe):
                for i, (b0, n) in enumerate(banks):
                    pe.wait_ge(normalised, i + 1)
                    if i >= 4:
                        pe.wait_ge(copied, i - 3)
                    for k in range(n // 2):
                        c = (b0 // 2 + k) * P
                        m = nc.tensor.transpose(ps_n[i % 4][:, k * P:(k + 1) * P], total[:, c:c + P], ident[:])
                    m.then_inc(turned, 1)

            @b4.vector
            def _(dve):
                n_done = [0]

                def then(i):
                    n_done[0] += 1
                    i.then_inc(d, 1)
                    dve.wait_ge(d, n_done[0])

                dve.wait_ge(x_in, 64)

                def residual(i):
                    b0, n = banks[i]
                    dve.wait_ge(turned, i + 1)
                    nc.vector.scalar_tensor_tensor(
                        w[:, b0:b0 + n, :].rearrange("p b d -> p (b d)"),
                        x_s[:, b0:b0 + n, :].rearrange("p b d -> p (b d)"), 2.0,
                        ps_n[i % 4][:, 0:n * D], ALU.mult, ALU.add).then_inc(copied, 1)

                def centre(p):
                    b0, b1 = spans[p]
                    dve.wait_ge(copied, pieces[p][1])
                    then(nc.vector.tensor_reduce(ln[:, 0, b0:b1], w[:, b0:b1, :], AX.X, ALU.add))
                    then(nc.vector.tensor_scalar(ln[:, 1, b0:b1], ln[:, 0, b0:b1], 1.0 / D, None, ALU.mult))
                    nc.vector.tensor_tensor(v[:, b0:b1, :], w[:, b0:b1, :], wide(ln[:, 1, :], b0, b1),
                                            ALU.subtract).then_inc(centred, 1)

                def variance(p):
                    b0, b1 = spans[p]
                    dve.wait_ge(squared, p + 1)
                    nc.vector.tensor_reduce(ln[:, 0, b0:b1], w[:, b0:b1, :], AX.X, ALU.add).then_inc(spread, 1)
                    dve.wait_ge(spread, 2 * p + 1)
                    nc.vector.tensor_scalar(ln[:, 2, b0:b1], ln[:, 0, b0:b1], 1.0 / D, EPS,
                                            ALU.mult, ALU.add).then_inc(spread, 1)

                def invert(p):
                    b0, b1 = spans[p]
                    dve.wait_ge(rooted, p + 1)
                    nc.vector.reciprocal(ln[:, 4, b0:b1], ln[:, 3, b0:b1]).then_inc(inverted, 1)

                for p in range(len(pieces) + 1):
                    if p < len(pieces):
                        for i in range(*pieces[p]):
                            residual(i)
                    if p >= 1:
                        variance(p - 1)
                    if p < len(pieces):
                        centre(p)
                    if p >= 1:
                        invert(p - 1)


def kernel(x, src, dst, edge_attr_41, L0_gnn_W1, L0_gnn_b1, L0_gnn_W2, L0_gnn_b2, L0_gnn_g1, L0_gnn_bt1,
           L0_gnn_g2, L0_gnn_bt2, L0_gnn_g3, L0_gnn_bt3):
    import numpy as np
    import concourse.bacc as _bacc
    from concourse.bass_utils import run_bass_kernel_spmd as _run

    f = np.float32
    x, src, dst, ea, w1 = (np.asarray(a) for a in (x, src, dst, edge_attr_41, L0_gnn_W1))
    cols = [np.asarray(a) for a in (L0_gnn_g1, L0_gnn_bt1, L0_gnn_g2, L0_gnn_bt2, L0_gnn_g3, L0_gnn_bt3)]

    pad = PAD_EDGES - EDGES
    src_p = np.concatenate([src, np.zeros(pad, src.dtype)])
    dst_p = np.concatenate([dst, np.broadcast_to(dst[-1:], (pad,))])
    edge = np.zeros((SUPERS, KF - D, SUP), f)
    ea_p = np.concatenate([ea, np.zeros((pad, EF), f)]).reshape(SUPERS, SUP, EF)
    edge[:, 0:EF, :] = ea_p.transpose(0, 2, 1)
    edge[:, EF, :] = 1.0
    xT = np.zeros((D, 2 * XT_COLS), f)
    xT[:, 0:NODES] = x.T
    xT = np.ascontiguousarray(xT.reshape(D, -1, 2, P).transpose(2, 0, 1, 3)).reshape(2 * D, XT_COLS)
    w_dst = np.zeros((2, D, 2, D), f)
    w_dst[0, :, 0], w_dst[1, :, 1] = (w1[:, D:2 * D].T,) * 2
    w_edge = np.zeros((KF, D), f)
    w_edge[0:D] = w1[:, 0:D].T
    w_edge[D:D + EF] = w1[:, 2 * D:].T
    w_edge[D + EF] = np.asarray(L0_gnn_b1)
    low = (TILES // TS * GT + min(GT, LAST_TILES)) * P
    share = np.array([[low / EDGES, 0.5]] * D + [[(EDGES - low) / EDGES, 0.5]] * D, f)
    k = np.arange(P)
    arrays = {
        "xT": xT, "xn": x, "src_cols": np.ascontiguousarray(src_p.reshape(SUPERS, TS, P).transpose(0, 2, 1)),
        "dst_cols": np.ascontiguousarray(dst_p.reshape(ALL_TILES, P).T),
        "dst_rows": dst_p.reshape(ROUNDS, SR * SUP), "edgeT": edge, "w_edge": w_edge,
        "w_dst": w_dst.reshape(2 * D, 2 * D),
        "params": np.ascontiguousarray(np.stack([np.concatenate([c, c]) for c in cols], 1)),
        "wcol": share, "ident_in": np.eye(P, dtype=f), "fold_in": (k[:, None] % D == k[None, :] % D).astype(f),
        "nodecol_in": (k[:, None] + P * np.arange(NB)[None, :]).astype(f),
        "iota_in": np.broadcast_to(np.arange(WIN), (P, WIN)).astype(f),
    }
    nc = _bacc.Bacc("TRN2", target_bir_lowering=False, num_devices=1)
    args = [nc.dram_tensor(n, a.shape, mybir.dt.from_np(a.dtype), kind="ExternalInput").ap()
            for n, a in arrays.items()]
    args.append(nc.dram_tensor("out", (NODES, D), f32, kind="ExternalOutput").ap())
    gnn_kernel(nc, *args)
    r = _run(nc, [arrays], core_ids=[0])
    return r.results[0]["out"]
```
